# Optimizing a Trainium2 kernel written in Bass

```python
import numpy as np
import jax
import jax.numpy as jnp

def _softmax(x, axis=-1):
    return jax.nn.softmax(x, axis=axis)

def _gelu(x):
    return jax.nn.gelu(x, approximate=True)

def _silu(x):
    return jax.nn.silu(x)

def _sigmoid(x):
    return jax.nn.sigmoid(x)

def _layernorm(x, axis=-1, eps=1e-05):
    m = jnp.mean(x, axis=axis, keepdims=True)
    v = jnp.var(x, axis=axis, keepdims=True)
    return (x - m) / jnp.sqrt(v + eps)

def _scatter_add(tgt, idx, src, axis=0):
    return tgt.at[idx].add(src)

def _segment_sum(src, seg, n):
    return jax.ops.segment_sum(src, seg, n)
kernel_name = 'mk_seq_preln_d1_jaxref_r4_172ec9'

def setup_inputs(seed: int=0):
    np.random.seed(seed)
    _w = jnp.asarray

    def _L0_attn_setup():
        import jax, jax.numpy as jnp
        import numpy as np
        NUM_HEADS = 16
        key = jax.random.key(seed)
        ks = jax.random.split(key, 5)
        B, N, C = (4, 512, 256)
        s = 0.02
        return {'x': jax.random.normal(ks[0], (B, N, C), jnp.float32), 'w_qkv': jax.random.normal(ks[1], (C, 3 * C), jnp.float32) * s, 'b_qkv': jnp.zeros((3 * C,), jnp.float32), 'w_proj': jax.random.normal(ks[2], (C, C), jnp.float32) * s, 'b_proj': jnp.zeros((C,), jnp.float32)}
    _L0_attn_in = _L0_attn_setup()

    def _L0_ffn_setup():
        import jax, jax.numpy as jnp
        import numpy as np
        B, S, H = (4, 512, 256)
        E, K = (8, 2)
        I_R, I_S = (4 * H, 8 * H)
        CAP_FACTOR = 1.25
        SCALE = 1.0
        key = jax.random.key(seed)
        ks = jax.random.split(key, 9)
        std = 0.02
        return {'x': jax.random.normal(ks[0], (B, S, H), jnp.float32), 'router_w': std * jax.random.normal(ks[1], (E, H), jnp.float32), 'rg': std * jax.random.normal(ks[2], (E, H, I_R), jnp.float32), 'ru': std * jax.random.normal(ks[3], (E, H, I_R), jnp.float32), 'rd': std * jax.random.normal(ks[4], (E, I_R, H), jnp.float32), 'sg': std * jax.random.normal(ks[5], (H, I_S), jnp.float32), 'su': std * jax.random.normal(ks[6], (H, I_S), jnp.float32), 'sd': std * jax.random.normal(ks[7], (I_S, H), jnp.float32)}
    _L0_ffn_in = _L0_ffn_setup()
    _d = {'L0_attn_x': _L0_attn_in['x'], 'L0_attn_w_qkv': _L0_attn_in['w_qkv'], 'L0_attn_b_qkv': _L0_attn_in['b_qkv'], 'L0_attn_w_proj': _L0_attn_in['w_proj'], 'L0_attn_b_proj': _L0_attn_in['b_proj'], 'L0_ffn_router_w': _L0_ffn_in['router_w'], 'L0_ffn_rg': _L0_ffn_in['rg'], 'L0_ffn_ru': _L0_ffn_in['ru'], 'L0_ffn_rd': _L0_ffn_in['rd'], 'L0_ffn_sg': _L0_ffn_in['sg'], 'L0_ffn_su': _L0_ffn_in['su'], 'L0_ffn_sd': _L0_ffn_in['sd']}
    _x0 = _d['L0_attn_x']
    _d['L0_attn_x'] = jax.random.normal(jax.random.fold_in(jax.random.key(seed), 1), (8, 512, 256), dtype=_x0.dtype)
    del _x0
    return _d

def reference(L0_attn_x, L0_attn_w_qkv, L0_attn_b_qkv, L0_attn_w_proj, L0_attn_b_proj, L0_ffn_router_w, L0_ffn_rg, L0_ffn_ru, L0_ffn_rd, L0_ffn_sg, L0_ffn_su, L0_ffn_sd):

    def _L0_attn_ref(x, w_qkv, b_qkv, w_proj, b_proj):
        import jax, jax.numpy as jnp
        import numpy as np
        NUM_HEADS = 16
        B, N, C = x.shape
        H = NUM_HEADS
        D = C // H
        scale = D ** (-0.5)
        qkv = x @ w_qkv + b_qkv
        qkv = qkv.reshape(B, N, 3, H, D)
        q, k, v = (jnp.moveaxis(qkv, 2, 0)[i] for i in range(3))
        scores = jnp.einsum('bqhd,bkhd->bhqk', q.astype(jnp.float32), k.astype(jnp.float32)) * scale
        attn = jax.nn.softmax(scores, axis=-1).astype(q.dtype)
        out = jnp.einsum('bhqk,bkhd->bqhd', attn, v).reshape(B, N, C)
        return out @ w_proj + b_proj

    def _L0_ffn_ref(x, router_w, rg, ru, rd, sg, su, sd):
        import jax, jax.numpy as jnp
        import numpy as np
        B, S, H = (4, 512, 256)
        E, K = (8, 2)
        I_R, I_S = (4 * H, 8 * H)
        CAP_FACTOR = 1.25
        SCALE = 1.0
        b, s, h = x.shape
        T = b * s
        capacity = max(int(CAP_FACTOR * T / E), 1)
        xf = x.reshape(T, h)
        eps = jnp.finfo(x.dtype).eps
        xn = xf * jax.lax.rsqrt(jnp.mean(xf * xf, axis=-1, keepdims=True) + eps)
        logits = xn @ router_w.T
        probs = jax.nn.softmax(logits, axis=-1)
        topk_p, topk_i = jax.lax.top_k(probs, K)
        rw = topk_p / jnp.sum(topk_p, axis=-1, keepdims=True)
        one_hot = jax.nn.one_hot(topk_i, E, dtype=x.dtype)
        mask = one_hot.sum(1)
        wdense = (one_hot * rw[..., None]).sum(1)
        sel = mask.T.astype(bool)
        order = jnp.argsort(~sel, axis=1, stable=True)
        dispatch = order[:, :capacity]
        count = sel.sum(axis=1)
        valid = (jnp.arange(capacity)[None, :] < count[:, None]).astype(x.dtype)
        xg = xf[dispatch]
        gate = jax.nn.silu(jnp.einsum('ech,ehi->eci', xg, rg))
        up = jnp.einsum('ech,ehi->eci', xg, ru)
        eout = jnp.einsum('eci,eih->ech', gate * up, rd)
        w = jnp.take_along_axis(wdense.T, dispatch, axis=1)
        contrib = eout * (w * valid)[..., None]
        routed = jnp.zeros_like(xf).at[dispatch.reshape(-1)].add(contrib.reshape(-1, h))
        shared = jax.nn.silu(x @ sg) * (x @ su) @ sd
        return shared + SCALE * routed.reshape(b, s, h)
    x = L0_attn_x
    x = x + _L0_attn_ref(_layernorm(x, axis=-1), L0_attn_w_qkv, L0_attn_b_qkv, L0_attn_w_proj, L0_attn_b_proj)
    x = x + _L0_ffn_ref(_layernorm(x, axis=-1), L0_ffn_router_w, L0_ffn_rg, L0_ffn_ru, L0_ffn_rd, L0_ffn_sg, L0_ffn_su, L0_ffn_sd)
    return x

_drawn_inputs = setup_inputs


def setup_inputs(seed=0):
    import zlib

    import numpy as np

    out = dict(_drawn_inputs(seed))
    spreads = {'L0_attn_b_qkv': (0.0, 0.1), 'L0_attn_b_proj': (0.0, 0.1)}
    factors = {'L0_attn_w_qkv': 8.0,
     'L0_ffn_router_w': 3.384,
     'L0_ffn_rg': 3.016,
     'L0_ffn_ru': 2.978,
     'L0_ffn_rd': 2.975}
    for name, (base, spread) in spreads.items():
        noise = np.random.default_rng([zlib.crc32(name.encode()), seed]).standard_normal(out[name].shape)
        drawn = base * np.exp(spread * noise) if base else spread * noise
        out[name] = jnp.asarray(drawn.astype(out[name].dtype))
    for name, factor in factors.items():
        out[name] = (out[name] * factor).astype(out[name].dtype)
    return out
```

```python
from contextlib import ExitStack

import concourse.bass as bass
from concourse import mybir

F32 = mybir.dt.float32
F32R = mybir.dt.float32r
BF16 = mybir.dt.bfloat16
U32 = mybir.dt.uint32
ALU = mybir.AluOpType
ACT = mybir.ActivationFunctionType
AX = mybir.AxisListType

P = 128
NB, SEQ, C = 8, 512, 256
NH, HD = 16, 16
CT = C // P
TT = SEQ // P
KT = SEQ // P
GRP = 4
NG = NH // GRP
PAIRS = NH // 2
NE, IR, IS = 8, 4 * C, 8 * C
TOKENS = NB * SEQ
CAP = int(1.25 * TOKENS / NE)
SLOTS = NE * CAP
LN_EPS = 1e-5
RMS_EPS = 1.1920928955078125e-07
SCALE = HD ** -0.5
STACK = 4 * HD
ROWS_MAX = STACK + 1
ROWS_EXP = STACK + 3
FT = IR // P
XT_SLOTS, QK_SLOTS, V_SLOTS, PROJ_SLOTS = (2, 3), (4, 5, 13, 15), (6, 7), (8, 9)
ZERO_STORES = SLOTS // P // 4 + 1
DMA = 16

PIECES = 2 * FT
PIECE = 3 * CT * IR // PIECES


def piece_parts(n):
    parts, at, end = [], n * PIECE, (n + 1) * PIECE
    while at < end:
        k, off = divmod(at, CT * IR)
        m = min(end - at, CT * IR - off)
        parts.append((k, slice(off, off + m)))
        at += m
    return parts


PARTS_BEFORE = [sum(len(piece_parts(m)) for m in range(n)) for n in range(PIECES + 1)]
PARTS = PARTS_BEFORE[PIECES]


def count(eng, value):
    return max(value, 0) if isinstance(value, int) else eng.to_reg(value)


def counts(eng, *values):
    return [count(eng, v) for v in values]


def flat(tensor):
    return tensor[:].rearrange("p a b -> p (a b)")


def one_batch(view, n):
    return view[n] if isinstance(n, int) else view[bass.ds(n, 1)].rearrange("b p t c -> (b p) t c")


class Reader:

    def __init__(self):
        self.sem, self.value = None, 0

    def is_(self, sem, value):
        self.sem, self.value = sem, value


def attention_block(nc, x, w_qkv, b_qkv, w_proj, b_proj, router_w, sg, su, sd,
                    x1_dram, x2t_dram, slots_dram, rows_dram, recip_dram, keep):
    with ExitStack() as ctx:
        def sb(name, shape, dt=F32):
            return ctx.enter_context(nc.sbuf_tensor(name, shape, dt))

        def psum(name, cols):
            return ctx.enter_context(nc.psum_tensor(name, [P, cols], F32))

        def sem(name):
            return ctx.enter_context(nc.semaphore(name))

        ident = keep["ident"]
        before = sb("before", [P, P], BF16)
        ones = sb("ones", [P, P], BF16)
        expert_no = sb("expert_no", [P, TT, NE])
        rank = sb("rank", [P, TT, NE])
        minus_half = sb("minus_half", [P, TT])
        zeros = keep["raw"][0][1][:, 1, :]
        wq_raw = flat(keep["raw"][0][2])[:, 0:CT * 3 * C].rearrange("p (c n) -> p c n", c=CT)
        xs = keep["raw"][0][0][:, 0, :].rearrange("p (t c) -> p t c", t=TT)
        xn = keep["raw"][0][0][:, 1, :].rearrange("p (t c) -> p t c", t=TT)
        v_new = keep["raw"][0][1][:, 0, :].rearrange("p (t c) -> p t c", t=KT)
        q_st = keep["w_hi"][0][0][:].rearrange("p (h n) -> p h n", n=SEQ), keep["w_hi"][0][1][:].rearrange("p (h n) -> p h n", n=SEQ)
        k_st = keep["w_lo"][0][0][:].rearrange("p (h n) -> p h n", n=SEQ), keep["w_lo"][0][1][:].rearrange("p (h n) -> p h n", n=SEQ)
        qk_hi = keep["w_hi"][0][2][:].rearrange("p (m n) -> p m n", n=SEQ)
        qk_lo = keep["w_lo"][0][2][:].rearrange("p (m n) -> p m n", n=SEQ)
        wq_hi = sb("wq_hi", [P, CT, 3 * C], F32R)
        wq_lo = sb("wq_lo", [P, CT, 3 * C], F32R)
        wp = sb("wp", [P, NG, C])
        rw_raw = sb("rw_raw", [NE, C])
        rwt = sb("rwt", [P, CT, NE])
        bias_qk = sb("bias_qk", [P, 4])
        bias_v = sb("bias_v", [P, 2, C])
        st1 = sb("st1", [P, TT, 6])
        mv1 = sb("mv1", [P, TT, 2])
        rstd1 = sb("rstd1", [P, TT])
        xt_hi = sb("xt_hi", [P, CT, SEQ], F32R)
        xt_lo = sb("xt_lo", [P, CT, SEQ], F32R)
        v_aug = sb("v_aug", [P, KT, NH, 2 * HD])
        mx = sb("mx", [P, 2, 2 * TT])
        mt_hi = sb("mt_hi", [2 * TT, 2, P], F32R)
        mt_lo = sb("mt_lo", [2 * TT, 2, P], F32R)
        probs = sb("probs", [P, 2, GRP, KT, SEQ])
        o_sb = sb("o_sb", [P, 2, SEQ])
        den = sb("den", [P, HD])
        rden = sb("rden", [P, HD])
        r_wide = sb("r_wide", [P, SEQ])
        heads = sb("heads", [P, NG, SEQ])
        xr = sb("xr", [P, TT, C])
        st2 = sb("st2", [P, TT, 6])
        mv2 = sb("mv2", [P, TT, 2])
        rstd2 = sb("rstd2", [P, TT])
        xn2 = sb("xn2", [P, TT, C])
        sq = sb("sq", [P, C])
        ssq = sb("ssq", [P, TT])
        ms = sb("ms", [P, TT])
        rrms = sb("rrms", [P, TT])
        x2t = sb("x2t", [P, CT, SEQ])
        lg = sb("lg", [P, TT, NE])
        top = sb("top", [P, 2, TT])
        gap = sb("gap", [P, 2, TT])
        best = sb("best", [P, TT])
        key = sb("key", [P, TT, NE])
        chosen = sb("chosen", [P, 2, TT * NE])
        mask = sb("mask", [P, TT * NE], BF16)
        base = sb("base", [P, NE])
        pos = sb("pos", [P, TT, NE])
        slot_all = sb("slot_all", [P, TT, NE])
        picks = sb("picks", [P, 2, TT * NE])
        place = sb("place", [P, 2, TT])
        slot = sb("slot", [P, 2, TT])
        share = sb("share", [P, 2, TT])
        total = sb("total", [P, TT])
        row_no = sb("row_no", [P, 2, TT], U32)

        s_max = [psum(f"s_max{n}", SEQ) for n in range(2)]
        s_exp = [psum(f"s_exp{n}", 2 * SEQ) for n in range(2)]
        o_ps = psum("o_ps", SEQ)
        m_ps = psum("m_ps", SEQ)

        consts_made = sem("consts_made")
        dve_consts = sem("dve_consts")
        weights_loaded = sem("weights_loaded")
        rw_loaded = sem("rw_loaded")
        rwt_ready = sem("rwt_ready")
        rwt_copied = sem("rwt_copied")
        wq_hi_done = sem("wq_hi_done")
        wq_lo_done = sem("wq_lo_done")
        wp_zeroed = sem("wp_zeroed")
        wp_loaded = sem("wp_loaded")
        rows_zeroed = sem("rows_zeroed")
        x_loaded = sem("x_loaded")
        xr_loaded = sem("xr_loaded")
        ln1_steps = sem("ln1_steps")
        ln1_stats = sem("ln1_stats")
        ln1_rstd = sem("ln1_rstd")
        ln1_done = sem("ln1_done")
        xt_ready = sem("xt_ready")
        xt_hi_done = sem("xt_hi_done")
        xt_split = sem("xt_split")
        qk_ready = sem("qk_ready")
        qk_hi_done = sem("qk_hi_done")
        qk_split = sem("qk_split")
        v_ready = sem("v_ready")
        v_biased = sem("v_biased")
        v_copied = sem("v_copied")
        pair_loaded = [sem(f"pair_loaded{n}") for n in range(2)]
        s_max_ready = sem("s_max_ready")
        max_done = sem("max_done")
        mt_ready = sem("mt_ready")
        mt_hi_done = sem("mt_hi_done")
        mt_split = sem("mt_split")
        max_loaded = [sem(f"max_loaded{n}") for n in range(2)]
        s_exp_ready = sem("s_exp_ready")
        exp_done = sem("exp_done")
        pv_done = sem("pv_done")
        o_copied = sem("o_copied")
        den_loaded = sem("den_loaded")
        den_inverted = sem("den_inverted")
        recip_stored = sem("recip_stored")
        recip_loaded = sem("recip_loaded")
        heads_done = sem("heads_done")
        proj_ready = sem("proj_ready")
        x1_done = sem("x1_done")
        x1_stored = sem("x1_stored")
        ln2_steps = sem("ln2_steps")
        ln2_stats = sem("ln2_stats")
        ln2_rstd = sem("ln2_rstd")
        ln2_done = sem("ln2_done")
        ssq_done = sem("ssq_done")
        ms_done = sem("ms_done")
        rms_done = sem("rms_done")
        x2t_ready = sem("x2t_ready")
        x2t_copied = sem("x2t_copied")
        x2t_stored = sem("x2t_stored")
        logits_ready = sem("logits_ready")
        logits_read = sem("logits_read")
        choice_steps = sem("choice_steps")
        gap_known = sem("gap_known")
        gap_exp_done = sem("gap_exp_done")
        mask_done = sem("mask_done")
        pos_ready = sem("pos_ready")
        pos_read = sem("pos_read")
        slot_steps = sem("slot_steps")
        rows_known = sem("rows_known")
        rows_sent = sem("rows_sent")

        xv = x.rearrange("b (t p) c -> b p t c", p=P)
        x1v = x1_dram.rearrange("(b t p) c -> b p t c", p=P, t=TT)
        x2tv = x2t_dram.rearrange("(c p) t -> p c t", p=P)

        block = ctx.enter_context(nc.Block())

        @block.sync
        def _(sp):
            sp.dma_start(xs, xv[0]).then_inc(x_loaded, DMA)
            sp.dma_start(wq_raw, w_qkv.rearrange("(c p) n -> p c n", p=P)).then_inc(weights_loaded, DMA)
            for m in range(4):
                part, tile = m % 2, m // 2
                for pr in range(4):
                    for j in range(2):
                        first = part * C + tile * P + 32 * pr + HD * j
                        sp.dma_start(bias_qk[32 * pr + j:32 * pr + 32:2, m:m + 1],
                                     b_qkv[first:first + HD].rearrange("(d a) -> d a", a=1)).then_inc(weights_loaded, DMA)
            for t in range(2):
                sp.dma_start(bias_v[:, t, :], b_qkv[2 * C:3 * C].partition_broadcast(P)).then_inc(weights_loaded, DMA)
            sp.dma_start(rw_raw[:], router_w).then_inc(rw_loaded, DMA)
            sp.wait_ge(wp_zeroed, 1)
            wpv = w_proj.rearrange("(g j d) n -> j d g n", g=NG, j=GRP)
            for j in range(GRP):
                sp.dma_start(wp[32 * j:32 * j + HD, :, :], wpv[j]).then_inc(wp_loaded, DMA)
            sp.dma_start(wp[HD:HD + 1, 0, :], b_proj.rearrange("(a n) -> a n", a=1)).then_inc(wp_loaded, DMA)

            def load_pair(i, c):
                n, cc = i + c // PAIRS, c % PAIRS
                tile, row, half, ring = cc // 4, 32 * (cc % 4), (c % 4) // 2, 2 * (c % 2)
                tile_split, old_waited, old_used = counts(
                    sp, 4 * n + 2 * (tile + 1), 8 * (PAIRS * i + c) - 15, 4 * (PAIRS * i + c) - 12)
                sp.wait_ge(qk_split, tile_split)
                sp.wait_ge(s_max_ready, old_waited)
                sp.wait_ge(s_exp_ready, old_used)
                for r in range(4):
                    q_part = (qk_hi, qk_hi, qk_lo, qk_lo)[r]
                    k_part = (qk_hi, qk_lo, qk_hi, qk_lo)[r]
                    for to, part, m in ((q_st, q_part, 2 * tile), (k_st, k_part, 2 * tile + 1)):
                        sp.dma_start(to[half][HD * r:HD * r + HD, ring:ring + 2, :].bitcast(F32),
                                     part[row:row + 32, m, :].bitcast(F32)).then_inc(pair_loaded[c % 2], DMA)

            def load_max(i, c):
                half, ring = (c % 4) // 2, 2 * (c % 2)
                sp.wait_ge(mt_split, count(sp, PAIRS * i + c + 1))
                for r, part in enumerate((mt_hi, mt_lo)):
                    row = STACK + 1 + r
                    sp.dma_start(q_st[half][row:row + 1, ring:ring + 2, :].bitcast(F32),
                                 part[:, c % 2, :].bitcast(F32)).then_inc(max_loaded[c % 2], DMA)

            def load_den(i, g):
                sp.wait_ge(o_copied, count(sp, NG * i + g + 1))
                sp.dma_start(den[:], o_sb[HD:P:32, g % 2, :]).then_inc(den_loaded, DMA)

            def store_recip(i, g):
                sp.wait_ge(den_inverted, count(sp, NG * i + g + 1))
                sp.dma_start(recip_dram[g % 2].rearrange("j (a n) -> (j a) n", n=HD), rden[:]).then_inc(recip_stored, DMA)

            def load_recip(i, g):
                stored, used = counts(sp, DMA * (NG * i + g + 1), NG * i + g)
                sp.wait_ge(recip_stored, stored)
                sp.wait_ge(heads_done, used)
                sp.dma_start(r_wide[:], recip_dram[g % 2].rearrange("j (a n) -> j a n", a=1).to_broadcast([GRP, 32, SEQ])
                             ).then_inc(recip_loaded, DMA)

            def store_x1(n):
                sp.wait_ge(x1_done, count(sp, 2 * n + 2))
                sp.dma_start(one_batch(x1v, n), xr[:]).then_inc(x1_stored, DMA)

            def load_xr(n):
                read, stored = counts(sp, n, DMA * n)
                sp.wait_ge(ln2_done, read)
                sp.wait_ge(x1_stored, stored)
                sp.dma_start(xr[:], one_batch(xv, n)).then_inc(xr_loaded, DMA)

            def store_x2t(n):
                sp.wait_ge(x2t_copied, count(sp, CT * (n + 1)))
                sp.dma_start(x2tv[:, :, bass.ds(n * SEQ, SEQ)], x2t[:]).then_inc(x2t_stored, DMA)

            def load_x(n):
                sp.wait_ge(ln1_done, count(sp, n))
                sp.dma_start(xs, one_batch(xv, n)).then_inc(x_loaded, DMA)

            def body(i, first, last, more_x):
                for s in range(NH):
                    g, j = s // GRP, s % GRP
                    if s % 2 == 0:
                        if not (last and s // 2 + 3 >= PAIRS):
                            load_pair(i, s // 2 + 3)
                    if j == 0 and (not first or g >= 2):
                        load_den(i, g - 2)
                    if s % 2 == 0 and not (last and s // 2 + 1 >= PAIRS):
                        load_max(i, s // 2 + 1)
                    if not first or g >= 2:
                        if j == 1:
                            store_recip(i, g - 2)
                        if j == 2:
                            load_recip(i, g - 2)
                    if s == 3 and more_x:
                        load_x(i + 2)
                    if s == 10 and not first:
                        store_x1(i - 1)
                    if s == 12 and not first:
                        store_x2t(i - 1)
                    if s == 14:
                        load_xr(i)

            load_x(1)
            for c in range(3):
                load_pair(0, c)
            load_max(0, 0)
            body(0, True, False, True)
            with sp.Fori(1, NB - 2) as i:
                body(i, False, False, True)
            body(NB - 2, False, False, False)
            body(NB - 1, False, True, False)
            sp.wait_ge(v_copied, NG * NB)
            sp.wait_ge(xt_ready, CT * NB)
            sp.wait_ge(rows_zeroed, DMA * ZERO_STORES)
            for dst, src in zip(keep["raw"][0], (sg.rearrange("(c p) n -> p c n", p=P)[:, :, 0:IR],
                                                 su.rearrange("(c p) n -> p c n", p=P)[:, :, 0:IR],
                                                 sd.rearrange("(f p) n -> p f n", p=P)[:, 0:FT, :])):
                sp.dma_start(dst[:], src).then_inc(keep["raw_loaded"], DMA)
            for g in (2, 3):
                load_den(NB - 1, g)
                store_recip(NB - 1, g)
                load_recip(NB - 1, g)
            store_x1(NB - 1)
            store_x2t(NB - 1)
            sp.wait_ge(x1_stored, DMA * NB)
            sp.wait_ge(x2t_stored, DMA * NB)

        @block.gpsimd
        def _(pool):
            pool.memset(ident[:], 0.0).then_inc(consts_made, 1)
            pool.memset(before[:], 0.0).then_inc(consts_made, 1)
            pool.memset(zeros, 0.0).then_inc(consts_made, 1)
            pool.memset(ones[:], 1.0).then_inc(consts_made, 1)
            pool.memset(minus_half[:], -0.5).then_inc(consts_made, 1)
            pool.iota(expert_no[:], pattern=[[0, TT], [1, NE]], base=0, channel_multiplier=0,
                      allow_small_or_imprecise_dtypes=True).then_inc(consts_made, 1)
            pool.iota(rank[:], pattern=[[0, TT], [-1, NE]], base=NE, channel_multiplier=0,
                      allow_small_or_imprecise_dtypes=True).then_inc(consts_made, 1)
            pool.wait_ge(consts_made, 7)
            pool.affine_select(out=ident[:], in_=ident[:], compare_op=ALU.not_equal, fill=1.0, base=0,
                               pattern=[[-1, P]], channel_multiplier=1).then_inc(consts_made, 1)
            pool.affine_select(out=before[:], in_=before[:], compare_op=ALU.is_ge, fill=1.0, base=0,
                               pattern=[[-1, P]], channel_multiplier=1).then_inc(consts_made, 1)
            zv = slots_dram.rearrange("(n p r) c -> n p (r c)", p=P, r=4)
            for n in range(ZERO_STORES - 1):
                pool.dma_start(zv[n], zeros).then_inc(rows_zeroed, DMA)
            pool.dma_start(rows_dram[SLOTS:SLOTS + 1, :], zeros[0:1, 0:C]).then_inc(rows_zeroed, DMA)

            def rstd1_of(n):
                pool.wait_ge(ln1_stats, count(pool, n + 1))
                pool.tensor_tensor(rstd1[:], mv1[:, :, 1], minus_half[:], ALU.pow).then_inc(ln1_rstd, 1)

            def rstd2_of(n):
                pool.wait_ge(ln2_stats, count(pool, n + 1))
                pool.tensor_tensor(rstd2[:], mv2[:, :, 1], minus_half[:], ALU.pow).then_inc(ln2_rstd, 1)

            def rms_of(n):
                made, summed = counts(pool, 9, TT * (n + 1))
                pool.wait_ge(consts_made, made)
                pool.wait_ge(ssq_done, summed)
                pool.tensor_scalar(ms[:], ssq[:], 1.0 / C, RMS_EPS, ALU.mult, ALU.add).then_inc(ms_done, 1)
                pool.wait_ge(ms_done, count(pool, n + 1))
                pool.tensor_tensor(rrms[:], ms[:], minus_half[:], ALU.pow).then_inc(rms_done, 1)

            def normalise_heads(i, g):
                loaded, projected = counts(pool, DMA * (NG * i + g + 1), 2 * (i + g // NG))
                pool.wait_ge(recip_loaded, loaded)
                pool.wait_ge(proj_ready, projected)
                pool.tensor_tensor(heads[:, g % NG, :], o_sb[:, g % 2, :], r_wide[:], ALU.mult).then_inc(heads_done, 1)

            def dispatch(n):
                if isinstance(n, int) and n == 0:
                    pool.wait_ge(rows_zeroed, DMA * ZERO_STORES)
                made, known = counts(pool, 9, n + 1)
                pool.wait_ge(consts_made, made)
                pool.wait_ge(rows_known, known)
                for t in range(TT):
                    for k in range(2):
                        pool.indirect_dma_start(
                            slots_dram, bass.IndirectOffsetOnAxis(ap=row_no[:, k, t:t + 1], axis=0),
                            xn2[:, t, :], None, bounds_check=SLOTS - 1, oob_is_err=False).then_inc(rows_sent, DMA)

            def body(i, first, last):
                for g in range(NG):
                    if g == 0 and not last:
                        rstd1_of(i + 1)
                    if g == 2 and not first:
                        rstd2_of(i - 1)
                    if not first or g >= 2:
                        normalise_heads(i, g - 2)
                    if g == 2 and not first:
                        rms_of(i - 1)
                if not first:
                    dispatch(i - 1)

            rstd1_of(0)
            body(0, True, False)
            body(1, False, False)
            with pool.Fori(2, NB - 1) as i:
                body(i, False, False)
            body(NB - 1, False, True)
            normalise_heads(NB - 1, 2)
            normalise_heads(NB - 1, 3)
            rstd2_of(NB - 1)
            rms_of(NB - 1)
            dispatch(NB - 1)
            pool.wait_ge(rows_sent, DMA * 2 * TT * NB)

        @block.scalar
        def _(act):
            act.wait_ge(weights_loaded, DMA * 35)
            for c in range(CT):
                for part in range(2):
                    src = wq_raw[:, c, part * C:(part + 1) * C].rearrange("p (r j d) -> p r d j", j=2, d=HD)
                    dst = wq_hi[:, c, part * C:(part + 1) * C].rearrange("p (r d j) -> p r d j", j=2, d=HD)
                    act.activation(dst, src, ACT.Copy).then_inc(wq_hi_done, 1)
                act.activation(wq_hi[:, c, 2 * C:], wq_raw[:, c, 2 * C:], ACT.Copy).then_inc(wq_hi_done, 1)

            def xt_hi_part(n, c):
                act.wait_ge(xt_ready, count(act, CT * n + c + 1))
                act.activation(xt_hi[:, c, :], m_ps[:], ACT.Copy).then_inc(xt_hi_done, 1)

            def qk_hi_part(n, m):
                ready, left = counts(act, 4 * n + m + 1, 8 * (PAIRS * (n - 1) + 4 * (m // 2) + 3) + 1)
                act.wait_ge(qk_ready, ready)
                act.wait_ge(s_max_ready, left)
                act.activation(qk_hi[:, m, :], m_ps[:], ACT.Identity, bias=bias_qk[:, m:m + 1]).then_inc(qk_hi_done, 1)

            def mt_hi_part(i, c):
                ready, used = counts(act, PAIRS * i + c + 1, 4 * (PAIRS * i + c) - 7)
                act.wait_ge(mt_ready, ready)
                act.wait_ge(s_exp_ready, used)
                act.activation(mt_hi[:, c % 2, :], m_ps[0:2 * TT, 0:P], ACT.Copy).then_inc(mt_hi_done, 1)

            def exps(i, s, half):
                g = s // GRP
                ready, used = counts(act, 2 * (NH * i + s) + half + 1, NG * i + g - 1)
                act.wait_ge(s_exp_ready, ready)
                act.wait_ge(pv_done, used)
                act.activation(probs[:, g % 2, s % GRP, 2 * half:2 * half + 2, :],
                               s_exp[half][:].rearrange("p (k q) -> p k q", k=2), ACT.Exp,
                               scale=SCALE).then_inc(exp_done, 1)

            def copy_o(i, g):
                ready, used = counts(act, NG * i + g + 1, NG * i + g - 1)
                act.wait_ge(pv_done, ready)
                act.wait_ge(heads_done, used)
                act.activation(o_sb[:, g % 2, :], o_ps[:], ACT.Copy).then_inc(o_copied, 1)

            def squares(n):
                normal, read = counts(act, n + 1, n)
                act.wait_ge(ln2_done, normal)
                act.wait_ge(ms_done, read)
                for t in range(TT):
                    act.activation(sq[:], xn2[:, t, :], ACT.Square, accum_out=ssq[:, t:t + 1]).then_inc(ssq_done, 1)
                    act.wait_ge(ssq_done, count(act, TT * n + t + 1))

            def x2t_part(n, c):
                ready, stored, used = counts(act, CT * n + c + 1, DMA * n, n)
                act.wait_ge(x2t_ready, ready)
                act.wait_ge(x2t_stored, stored)
                act.wait_ge(logits_ready, used)
                act.activation(x2t[:, c, :], m_ps[:], ACT.Copy).then_inc(x2t_copied, 1)

            def gap_exp(n):
                act.wait_ge(gap_known, count(act, n + 1))
                act.activation(gap[:, 1, :], gap[:, 0, :], ACT.Exp).then_inc(gap_exp_done, 1)

            def body(i, first, last):
                for s in range(NH):
                    g = s // GRP
                    if s % GRP == 0 and (not first or g >= 2):
                        copy_o(i, g - 2)
                    if s == 12 and not first:
                        x2t_part(i - 1, 1)
                    if s % 2 == 0 and not (last and s == 14):
                        mt_hi_part(i, s // 2 + 1)
                    exps(i, s, 0)
                    if not last:
                        if s in XT_SLOTS:
                            xt_hi_part(i + 1, XT_SLOTS.index(s))
                        if s in QK_SLOTS:
                            qk_hi_part(i + 1, QK_SLOTS.index(s))
                    if not first:
                        if s == 11:
                            x2t_part(i - 1, 0)
                        if s == 14:
                            gap_exp(i - 1)
                    exps(i, s, 1)
                    if s == 11 and not first:
                        squares(i - 1)

            xt_hi_part(0, 0)
            xt_hi_part(0, 1)
            for m in range(4):
                qk_hi_part(0, m)
            mt_hi_part(0, 0)
            body(0, True, False)
            with act.Fori(1, NB - 1) as i:
                body(i, False, False)
            body(NB - 1, False, True)
            copy_o(NB - 1, 2)
            copy_o(NB - 1, 3)
            act.wait_ge(s_exp_ready, 2 * NH * NB)
            act.wait_ge(keep["raw_loaded"], 3 * DMA)
            for n in range(PIECES):
                for k, cols in piece_parts(n):
                    act.activation(keep["w_hi"][0][k][:, cols], flat(keep["raw"][0][k])[:, cols],
                                   ACT.Copy).then_inc(keep["w_hi_done"], 1)
            squares(NB - 1)
            x2t_part(NB - 1, 0)
            x2t_part(NB - 1, 1)
            gap_exp(NB - 1)

        @block.vector
        def _(dve):
            dve.memset(wp[:], 0.0).then_inc(wp_zeroed, 1)
            for h in range(2):
                dve.memset(q_st[h][STACK:STACK + 32, :, :].bitcast(F32), 0.0).then_inc(dve_consts, 1)
                dve.memset(k_st[h][STACK:STACK + 32, :, :].bitcast(F32), -1.0).then_inc(dve_consts, 1)
            dve.memset(v_aug[:], 1.0).then_inc(dve_consts, 1)
            dve.memset(base[:], 0.0).then_inc(dve_consts, 1)

            def ln_stats(n, src, st, mv, steps, stats):
                for t in range(TT):
                    dve.bn_stats(st[:, t, :], src[:, t, :]).then_inc(steps, 1)
                made, known = counts(dve, 6, 2 * TT * n + TT)
                dve.wait_ge(dve_consts, made)
                dve.wait_ge(steps, known)
                for t in range(TT):
                    dve.bn_aggr(mv[:, t, :], st[:, t, :]).then_inc(steps, 1)
                dve.wait_ge(steps, count(dve, 2 * TT * n + 2 * TT))
                dve.tensor_scalar(mv[:, :, 1], mv[:, :, 1], LN_EPS, None, ALU.add).then_inc(stats, 1)

            def ln1_a(n):
                dve.wait_ge(x_loaded, count(dve, DMA * (n + 1)))
                ln_stats(n, xs, st1, mv1, ln1_steps, ln1_stats)

            def ln1_b(n):
                dve.wait_ge(ln1_rstd, count(dve, n + 1))
                for t in range(TT):
                    ins = dve.tensor_scalar(xn[:, t, :], xs[:, t, :], mv1[:, t, 0:1], rstd1[:, t:t + 1],
                                            ALU.subtract, ALU.mult)
                ins.then_inc(ln1_done, 1)

            def xt_lo_part(n, c):
                dve.wait_ge(xt_hi_done, count(dve, CT * n + c + 1))
                dve.tensor_tensor(xt_lo[:, c, :], m_ps[:], xt_hi[:, c, :].bitcast(F32),
                                  ALU.subtract).then_inc(xt_split, 1)

            def qk_lo_part(n, m):
                dve.wait_ge(qk_hi_done, count(dve, 4 * n + m + 1))
                dve.scalar_tensor_tensor(out=qk_lo[:, m, :], in0=m_ps[:], scalar=bias_qk[:, m:m + 1],
                                         in1=qk_hi[:, m, :].bitcast(F32), op0=ALU.add,
                                         op1=ALU.subtract).then_inc(qk_split, 1)

            def v_part(n, t):
                ready, copied = counts(dve, 2 * n + t + 1, NG * n)
                dve.wait_ge(v_ready, ready)
                dve.wait_ge(v_copied, copied)
                dve.tensor_tensor(v_new[:, 2 * t:2 * t + 2, :], m_ps[:].rearrange("p (t c) -> p t c", t=2),
                                  bias_v[:], ALU.add).then_inc(v_biased, 1)

            def v_copy(n, g):
                biased, used = counts(dve, 2 * n + 2, NG * n + g - 3)
                dve.wait_ge(v_biased, biased)
                dve.wait_ge(pv_done, used)
                dve.tensor_copy(v_aug[:, :, GRP * g:GRP * g + GRP, 0:HD],
                                v_new[:, :, 64 * g:64 * g + 64].rearrange("p t (h d) -> p t h d", h=GRP)
                                ).then_inc(v_copied, 1)

            def row_max(i, s, q):
                dve.wait_ge(s_max_ready, count(dve, TT * (NH * i + s) + q + 1))
                dve.tensor_reduce(mx[:, (s // 2) % 2, TT * (s % 2) + q:TT * (s % 2) + q + 1], s_max[q % 2][:],
                                  AX.X, ALU.max).then_inc(max_done, 1)

            def mt_lo_part(i, c):
                dve.wait_ge(mt_hi_done, count(dve, PAIRS * i + c + 1))
                dve.tensor_tensor(mt_lo[:, c % 2, :], m_ps[0:2 * TT, 0:P], mt_hi[:, c % 2, :].bitcast(F32),
                                  ALU.subtract).then_inc(mt_split, 1)

            def invert_den(i, g):
                loaded, stored = counts(dve, DMA * (NG * i + g + 1), DMA * (NG * i + g))
                dve.wait_ge(den_loaded, loaded)
                dve.wait_ge(recip_stored, stored)
                dve.reciprocal(rden[:], den[:]).then_inc(den_inverted, 1)

            def add_x(n, t):
                ready, loaded = counts(dve, 2 * n + t + 1, DMA * (n + 1))
                dve.wait_ge(proj_ready, ready)
                dve.wait_ge(xr_loaded, loaded)
                part = xr[:, 2 * t:2 * t + 2, :]
                dve.tensor_tensor(part, m_ps[:].rearrange("p (t c) -> p t c", t=2), part, ALU.add).then_inc(x1_done, 1)

            def ln2_a(n):
                dve.wait_ge(x1_done, count(dve, 2 * n + 2))
                ln_stats(n, xr, st2, mv2, ln2_steps, ln2_stats)

            def ln2_b(n):
                ready, sent = counts(dve, n + 1, DMA * 2 * TT * n)
                dve.wait_ge(ln2_rstd, ready)
                dve.wait_ge(rows_sent, sent)
                for t in range(TT):
                    ins = dve.tensor_scalar(xn2[:, t, :], xr[:, t, :], mv2[:, t, 0:1], rstd2[:, t:t + 1],
                                            ALU.subtract, ALU.mult)
                ins.then_inc(ln2_done, 1)

            def over_experts(ap):
                return ap.rearrange("p (t a) -> p t a", a=1).to_broadcast([P, TT, NE])

            def for_both(tensor):
                return tensor[:].rearrange("p (a t) e -> p a (t e)", a=1).to_broadcast([P, 2, TT * NE])

            def by_expert(ap):
                return ap.rearrange("p (t e) -> p t e", e=NE)

            def choose(n):
                ready, known = counts(dve, n + 1, n + 1)
                dve.wait_ge(logits_ready, ready)
                dve.wait_ge(rms_done, known)
                dve.tensor_tensor(lg[:], by_expert(m_ps[:, 0:TT * NE]), over_experts(rrms[:]),
                                  ALU.mult).then_inc(logits_read, 1)
                dve.wait_ge(logits_read, count(dve, n + 1))
                for k in range(2):
                    done = CHOICE_STEPS * n + 6 * k
                    dve.tensor_reduce(top[:, k, :], lg[:], AX.X, ALU.max).then_inc(choice_steps, 1)
                    dve.wait_ge(choice_steps, count(dve, done + 1))
                    dve.tensor_tensor(key[:], lg[:], over_experts(top[:, k, :]), ALU.is_equal).then_inc(choice_steps, 1)
                    dve.wait_ge(choice_steps, count(dve, done + 2))
                    dve.tensor_tensor(key[:], key[:], rank[:], ALU.mult).then_inc(choice_steps, 1)
                    dve.wait_ge(choice_steps, count(dve, done + 3))
                    dve.tensor_reduce(best[:], key[:], AX.X, ALU.max).then_inc(choice_steps, 1)
                    dve.wait_ge(choice_steps, count(dve, done + 4))
                    dve.tensor_tensor(by_expert(chosen[:, k, :]), key[:], over_experts(best[:]),
                                      ALU.is_equal).then_inc(choice_steps, 1)
                    dve.wait_ge(choice_steps, count(dve, done + 5))
                    if k == 0:
                        dve.scalar_tensor_tensor(out=lg[:], in0=by_expert(chosen[:, 0, :]), scalar=-3.0e38, in1=lg[:],
                                                 op0=ALU.mult, op1=ALU.add).then_inc(choice_steps, 1)
                        dve.wait_ge(choice_steps, count(dve, done + 6))
                dve.tensor_tensor(mask[:], chosen[:, 0, :], chosen[:, 1, :], ALU.add).then_inc(mask_done, 1)
                dve.tensor_tensor(gap[:, 0, :], top[:, 1, :], top[:, 0, :], ALU.subtract).then_inc(gap_known, 1)

            CHOICE_STEPS = 11

            def number(n):
                done = SLOT_STEPS * n
                dve.wait_ge(pos_ready, count(dve, n + 1))
                for t in range(TT):
                    dve.tensor_tensor(pos[:, t, :], m_ps[:, NE * t:NE * t + NE], base[:], ALU.add).then_inc(slot_steps, 1)
                    dve.tensor_tensor(base[:], base[:], m_ps[:, NE * (TT + t):NE * (TT + t) + NE],
                                      ALU.add).then_inc(slot_steps, 1)
                    done = done + 2
                    dve.wait_ge(slot_steps, count(dve, done))
                dve.scalar_tensor_tensor(out=slot_all[:], in0=expert_no[:], scalar=float(CAP), in1=pos[:],
                                         op0=ALU.mult, op1=ALU.add).then_inc(pos_read, 1)
                dve.wait_ge(pos_read, count(dve, n + 1))
                dve.tensor_tensor(picks[:], chosen[:], for_both(pos), ALU.mult).then_inc(slot_steps, 1)
                dve.wait_ge(slot_steps, count(dve, done + 1))
                dve.tensor_reduce(place[:], picks[:].rearrange("p k (t e) -> p k t e", e=NE), AX.X,
                                  ALU.add).then_inc(slot_steps, 1)
                dve.wait_ge(slot_steps, count(dve, done + 2))
                dve.tensor_tensor(picks[:], chosen[:], for_both(slot_all), ALU.mult).then_inc(slot_steps, 1)
                dve.wait_ge(slot_steps, count(dve, done + 3))
                dve.tensor_reduce(slot[:], picks[:].rearrange("p k (t e) -> p k t e", e=NE), AX.X,
                                  ALU.add).then_inc(slot_steps, 1)
                dve.tensor_scalar(place[:], place[:], float(CAP), None, ALU.is_lt).then_inc(slot_steps, 1)
                dve.wait_ge(slot_steps, count(dve, done + 5))
                dve.scalar_tensor_tensor(out=slot[:], in0=slot[:], scalar=-float(SLOTS), in1=place[:],
                                         op0=ALU.add, op1=ALU.mult).then_inc(slot_steps, 1)
                dve.wait_ge(slot_steps, count(dve, done + 6))
                dve.tensor_scalar(slot[:], slot[:], float(SLOTS), None, ALU.add).then_inc(slot_steps, 1)
                sent, last = counts(dve, DMA * 2 * TT * n, done + 7)
                dve.wait_ge(rows_sent, sent)
                dve.wait_ge(slot_steps, last)
                dve.tensor_copy(row_no[:], slot[:]).then_inc(rows_known, 1)
                dve.tensor_copy(keep["row_no"][:, bass.ds(n, 1), :, :].rearrange("p n k t -> p (n k) t"),
                                slot[:]).then_inc(slot_steps, 1)
                dve.wait_ge(gap_exp_done, count(dve, n + 1))
                dve.tensor_scalar(total[:], gap[:, 1, :], 1.0, None, ALU.add).then_inc(slot_steps, 1)
                dve.wait_ge(slot_steps, count(dve, done + 9))
                dve.reciprocal(share[:, 0, :], total[:]).then_inc(slot_steps, 1)
                dve.wait_ge(slot_steps, count(dve, done + 10))
                dve.tensor_tensor(share[:, 1, :], gap[:, 1, :], share[:, 0, :], ALU.mult).then_inc(slot_steps, 1)
                dve.wait_ge(slot_steps, count(dve, done + 11))
                dve.tensor_tensor(keep["choice_w"][:, bass.ds(n, 1), :, :].rearrange("p n k t -> p (n k) t"),
                                  share[:], place[:], ALU.mult).then_inc(slot_steps, 1)

            SLOT_STEPS = 2 * TT + 12

            def body(i, first, last):
                for s in range(NH):
                    g, j = s // GRP, s % GRP
                    later_max = not (last and s + GRP >= NH)
                    if later_max:
                        row_max(i, s + GRP, 0)
                        row_max(i, s + GRP, 1)
                    if s % 2 == 0 and not (last and s == 14):
                        mt_lo_part(i, s // 2 + 1)
                    if j == 1 and (not first or g >= 2):
                        invert_den(i, g - 2)
                    if later_max:
                        row_max(i, s + GRP, 2)
                        row_max(i, s + GRP, 3)
                    if not last:
                        if s in XT_SLOTS:
                            xt_lo_part(i + 1, XT_SLOTS.index(s))
                        if s in QK_SLOTS:
                            qk_lo_part(i + 1, QK_SLOTS.index(s))
                        if s in V_SLOTS:
                            v_part(i + 1, V_SLOTS.index(s))
                        if s == 0:
                            ln1_a(i + 1)
                        if s == 1:
                            ln1_b(i + 1)
                    if not first:
                        if s == 1:
                            for gg in range(3):
                                v_copy(i, gg)
                        if s == 5:
                            v_copy(i, 3)
                        if s in PROJ_SLOTS:
                            add_x(i - 1, PROJ_SLOTS.index(s))
                        if s == 9:
                            ln2_a(i - 1)
                        if s == 10:
                            ln2_b(i - 1)
                        if s == 12:
                            choose(i - 1)
                        if s == 14:
                            number(i - 1)

            ln1_a(0)
            ln1_b(0)
            for c in range(CT):
                for part in range(2):
                    dve.wait_ge(wq_hi_done, 3 * c + part + 1)
                    src = wq_raw[:, c, part * C:(part + 1) * C].rearrange("p (r j d) -> p r d j", j=2, d=HD)
                    hi = wq_hi[:, c, part * C:(part + 1) * C].rearrange("p (r d j) -> p r d j", j=2, d=HD)
                    lo = wq_lo[:, c, part * C:(part + 1) * C].rearrange("p (r d j) -> p r d j", j=2, d=HD)
                    dve.tensor_tensor(lo, src, hi.bitcast(F32), ALU.subtract).then_inc(wq_lo_done, 1)
                dve.wait_ge(wq_hi_done, 3 * c + 3)
                dve.tensor_tensor(wq_lo[:, c, 2 * C:], wq_raw[:, c, 2 * C:], wq_hi[:, c, 2 * C:].bitcast(F32),
                                  ALU.subtract).then_inc(wq_lo_done, 1)
            dve.wait_ge(rwt_ready, 1)
            dve.tensor_copy(rwt[:], m_ps[:, 0:CT * NE].rearrange("p (c e) -> p c e", c=CT)).then_inc(rwt_copied, 1)
            dve.wait_ge(weights_loaded, DMA * 35)
            xt_lo_part(0, 0)
            xt_lo_part(0, 1)
            for m in range(4):
                qk_lo_part(0, m)
            v_part(0, 0)
            v_part(0, 1)
            dve.wait_ge(dve_consts, 6)
            for g in range(NG):
                v_copy(0, g)
            for s in range(GRP):
                for q in range(TT):
                    row_max(0, s, q)
                if s == 1:
                    mt_lo_part(0, 0)
            body(0, True, False)
            with dve.Fori(1, NB - 1) as i:
                body(i, False, False)
            body(NB - 1, False, True)
            invert_den(NB - 1, 2)
            invert_den(NB - 1, 3)
            for n in range(PIECES):
                for m, (k, cols) in enumerate(piece_parts(n)):
                    dve.wait_ge(keep["w_hi_done"], PARTS_BEFORE[n] + m + 1)
                    dve.tensor_tensor(keep["w_lo"][0][k][:, cols], flat(keep["raw"][0][k])[:, cols],
                                      keep["w_hi"][0][k][:, cols].bitcast(F32), ALU.subtract).then_inc(keep["w_split"], 1)
            add_x(NB - 1, 0)
            add_x(NB - 1, 1)
            ln2_a(NB - 1)
            ln2_b(NB - 1)
            choose(NB - 1)
            number(NB - 1)

        @block.tensor
        def _(pe):
            bank = Reader()

            def front_xt(n, c):
                ready, emptied = counts(pe, n + 1, bank.value)
                pe.wait_ge(ln1_done, ready)
                pe.wait_ge(bank.sem, emptied)
                for t in range(TT):
                    ins = pe.transpose(m_ps[:, P * t:P * t + P], xn[:, t, P * c:P * c + P], ident[:])
                ins.then_inc(xt_ready, 1)
                bank.is_(xt_split, CT * n + c + 1)

            def front_qk(n, m):
                split, emptied = counts(pe, CT * n + CT, bank.value)
                pe.wait_ge(xt_split, split)
                pe.wait_ge(bank.sem, emptied)
                cols = slice((m % 2) * C + (m // 2) * P, (m % 2) * C + (m // 2) * P + P)
                parts = [(w[:, c, cols], xp[:, c, :]) for c in range(CT)
                         for w, xp in ((wq_hi, xt_hi), (wq_hi, xt_lo), (wq_lo, xt_hi))]
                for k, (w, xp) in enumerate(parts):
                    ins = pe.matmul(m_ps[:], w, xp, start=(k == 0), stop=(k == len(parts) - 1))
                ins.then_inc(qk_ready, 1)
                bank.is_(qk_split, 4 * n + m + 1)

            def front_v(n, h):
                pe.wait_ge(bank.sem, count(pe, bank.value))
                for t in (2 * h, 2 * h + 1):
                    out = m_ps[:, C * (t % 2):C * (t % 2) + C]
                    parts = [(xp[:, c, P * t:P * t + P], w[:, c, 2 * C:]) for c in range(CT)
                             for xp, w in ((xt_hi, wq_hi), (xt_hi, wq_lo), (xt_lo, wq_hi))]
                    for k, (xp, w) in enumerate(parts):
                        ins = pe.matmul(out, xp, w, start=(k == 0), stop=(k == len(parts) - 1))
                ins.then_inc(v_ready, 1)
                bank.is_(v_biased, 2 * n + h + 1)

            def scores_max(i, s, q):
                reduced, loaded = counts(pe, TT * (NH * i + s) + q - 1,
                                         8 * DMA * ((PAIRS // 2) * i + s // 4 + 1))
                if q == 0 and s % 2 == 0:
                    pe.wait_ge(pair_loaded[(s // 2) % 2], loaded)
                pe.wait_ge(max_done, reduced)
                half, ring = (s // 4) % 2, s % 4
                pe.matmul(s_max[q % 2][:], q_st[half][0:ROWS_MAX, ring, P * q:P * q + P],
                          k_st[half][0:ROWS_MAX, ring, :], start=True, stop=True).then_inc(s_max_ready, 1)

            def scores_exp(i, s, k):
                if k % 2 == 0:
                    read, loaded = counts(pe, 2 * (NH * i + s) + k // 2 - 1,
                                          2 * DMA * ((PAIRS // 2) * i + s // 4 + 1))
                    if k == 0 and s % 2 == 0:
                        pe.wait_ge(max_loaded[(s // 2) % 2], loaded)
                    pe.wait_ge(exp_done, read)
                half, ring = (s // 4) % 2, s % 4
                ins = pe.matmul(s_exp[k // 2][:, SEQ * (k % 2):SEQ * (k % 2) + SEQ],
                                k_st[half][0:ROWS_EXP, ring, P * k:P * k + P],
                                q_st[half][0:ROWS_EXP, ring, :], start=True, stop=True)
                if k % 2 == 1:
                    ins.then_inc(s_exp_ready, 1)

            def pv(i, g, k):
                if k == 0:
                    probs_made, v_there, emptied = counts(pe, 2 * GRP * (NG * i + g + 1), NG * i + g + 1, NG * i + g)
                    pe.wait_ge(exp_done, probs_made)
                    pe.wait_ge(v_copied, v_there)
                    pe.wait_ge(o_copied, emptied)
                for j in range(GRP):
                    ins = pe.matmul(o_ps[32 * j:32 * j + 32, :], v_aug[:, k, (GRP * g + j) % NH, :],
                                    probs[:, g % 2, j, k, :], start=(k == 0), stop=(k == KT - 1))
                if k == KT - 1:
                    ins.then_inc(pv_done, 1)

            def max_t(i, c):
                reduced, emptied = counts(pe, 2 * TT * (PAIRS * i + c + 1), bank.value)
                pe.wait_ge(max_done, reduced)
                pe.wait_ge(bank.sem, emptied)
                pe.transpose(m_ps[0:2 * TT, 0:P], mx[:, c % 2, :], ident[:]).then_inc(mt_ready, 1)
                bank.is_(mt_split, PAIRS * i + c + 1)

            def project(n, h):
                normal, emptied = counts(pe, NG * n + NG, bank.value)
                pe.wait_ge(heads_done, normal)
                pe.wait_ge(bank.sem, emptied)
                for t in (2 * h, 2 * h + 1):
                    for g in range(NG):
                        ins = pe.matmul(m_ps[:, C * (t % 2):C * (t % 2) + C], heads[:, g, P * t:P * t + P],
                                        wp[:, g, :], start=(g == 0), stop=(g == NG - 1))
                ins.then_inc(proj_ready, 1)
                bank.is_(x1_done, 2 * n + h + 1)

            def back_xt(n, c):
                normal, emptied = counts(pe, n + 1, bank.value)
                pe.wait_ge(ln2_done, normal)
                pe.wait_ge(bank.sem, emptied)
                for t in range(TT):
                    ins = pe.transpose(m_ps[:, P * t:P * t + P], xn2[:, t, P * c:P * c + P], ident[:])
                ins.then_inc(x2t_ready, 1)
                bank.is_(x2t_copied, CT * n + c + 1)

            def logits(n):
                copied, emptied = counts(pe, CT * n + CT, bank.value)
                pe.wait_ge(x2t_copied, copied)
                pe.wait_ge(bank.sem, emptied)
                for t in range(TT):
                    for c in range(CT):
                        ins = pe.matmul(m_ps[:, NE * t:NE * t + NE], x2t[:, c, P * t:P * t + P], rwt[:, c, :],
                                        start=(c == 0), stop=(c == CT - 1))
                ins.then_inc(logits_ready, 1)
                bank.is_(logits_read, n + 1)

            def positions(n):
                known, emptied = counts(pe, n + 1, bank.value)
                pe.wait_ge(mask_done, known)
                pe.wait_ge(bank.sem, emptied)
                pe.matmul(m_ps[:, 0:TT * NE], before[:], mask[:], start=True, stop=True)
                pe.matmul(m_ps[:, TT * NE:2 * TT * NE], ones[:], mask[:], start=True, stop=True).then_inc(pos_ready, 1)
                bank.is_(pos_read, n + 1)

            def body(i, first, last):
                for s in range(NH):
                    if s == 12 and not first:
                        back_xt(i - 1, 1)
                    for q in range(TT):
                        if q == 2:
                            if s % 2 == 0 and not (last and s == 14):
                                max_t(i, s // 2 + 1)
                            if not (first and s < GRP):
                                pv(i, s // GRP - 1, s % GRP)
                            if not last:
                                if s in XT_SLOTS:
                                    front_xt(i + 1, XT_SLOTS.index(s))
                                if s in QK_SLOTS:
                                    front_qk(i + 1, QK_SLOTS.index(s))
                                if s in V_SLOTS:
                                    front_v(i + 1, V_SLOTS.index(s))
                            if not first:
                                if s in PROJ_SLOTS:
                                    project(i - 1, PROJ_SLOTS.index(s))
                                if s == 11:
                                    back_xt(i - 1, 0)
                                if s == 12:
                                    logits(i - 1)
                                if s == 14:
                                    positions(i - 1)
                        if not (last and s + GRP >= NH):
                            scores_max(i, s + GRP, q)
                        scores_exp(i, s, q)

            pe.wait_ge(consts_made, 9)
            pe.wait_ge(rw_loaded, DMA)
            for c in range(CT):
                ins = pe.transpose(m_ps[:, NE * c:NE * c + NE], rw_raw[:, P * c:P * c + P], ident[0:NE, 0:NE])
            ins.then_inc(rwt_ready, 1)
            bank.is_(rwt_copied, 1)
            front_xt(0, 0)
            front_xt(0, 1)
            pe.wait_ge(wq_lo_done, 3 * CT)
            for m in range(4):
                front_qk(0, m)
            front_v(0, 0)
            front_v(0, 1)
            pe.wait_ge(dve_consts, 6)
            for s in range(GRP):
                for q in range(TT):
                    scores_max(0, s, q)
                if s == 1:
                    max_t(0, 0)
            pe.wait_ge(wp_loaded, 5 * DMA)
            body(0, True, False)
            with pe.Fori(1, NB - 1) as i:
                bank.is_(qk_split, 4 * i + 4)
                body(i, False, False)
            bank.is_(qk_split, 4 * (NB - 1) + 4)
            body(NB - 1, False, True)
            for k in range(KT):
                pv(NB - 1, NG - 1, k)
            project(NB - 1, 0)
            project(NB - 1, 1)
            back_xt(NB - 1, 0)
            back_xt(NB - 1, 1)
            logits(NB - 1)
            positions(NB - 1)


TILE = SEQ
SPLIT = (384, 256)
E0, Z0 = NB, NB + 2 * NE
END = Z0 + NB


class Tile:

    def __init__(self, kind, index, half=0, odd=0):
        self.kind, self.index, self.half = kind, index, half
        if kind == "first":
            self.no, self.job, self.set, self.cols = index, 0, 0, TILE
        elif kind == "expert":
            self.no, self.job, self.set, self.cols = E0 + 2 * index + half, 1 + index, 1 - odd, SPLIT[half]
        else:
            self.no, self.job, self.set, self.cols = Z0 + index, 1 + NE, (1 + NE) % 2, TILE
        self.rows = self.cols // P


def all_tiles(eng, tile):
    def firsts(n, first, last):
        a, b = Tile("first", 2 * n), Tile("first", 2 * n + 1)
        tile(None if first else Tile("first", 2 * n - 1), a, b, 0, (), None)
        tile(a, b, Tile("expert", 0) if last else Tile("first", 2 * n + 2), 1, range(PIECES) if last else (), 1)

    def experts(n, first, last):
        before = Tile("first", NB - 1) if first else Tile("expert", 2 * n - 1, 1, 1)
        for odd in range(2):
            e = 2 * n + odd
            a, b = Tile("expert", e, 0, odd), Tile("expert", e, 1, odd)
            after = Tile("last", 0) if last and odd else Tile("expert", e + 1, 0, 1 - odd)
            tile(before, a, b, 0, range(0, PIECES // 2), e + 2)
            tile(a, b, after, 1, range(PIECES // 2, PIECES), e + 2)
            before = b

    def lasts(n, first, last):
        a, b = Tile("last", 2 * n), Tile("last", 2 * n + 1)
        tile(Tile("expert", NE - 1, 1, 1) if first else Tile("last", 2 * n - 1), a, b, 0, (), None)
        tile(a, b, None if last else Tile("last", 2 * n + 2), 1, (), None)

    for part, turns in ((firsts, NB // 2), (experts, NE // 2), (lasts, NB // 2)):
        part(0, True, False)
        with eng.Fori(1, turns - 1) as n:
            part(n, False, False)
        part(turns - 1, False, True)


def ffn_block(nc, sg, su, sd, rg, ru, rd, x1_dram, x2t_dram, slots_dram, rows_dram, keep, out):
    assert sum(SPLIT) == CAP and NB % 2 == 0 and NE % 2 == 0
    with ExitStack() as ctx:
        def sb(name, shape, dt=F32):
            return ctx.enter_context(nc.sbuf_tensor(name, shape, dt))

        def psum(name, cols):
            return ctx.enter_context(nc.psum_tensor(name, [P, cols], F32))

        def sem(name):
            return ctx.enter_context(nc.semaphore(name))

        ident = keep["ident"]
        raw = [keep["raw"][0], [sb("raw1_g", [P, CT, IR]), sb("raw1_u", [P, CT, IR]), sb("raw1_d", [P, FT, C])]]
        w_hi = [keep["w_hi"][0], [sb(f"w_hi1_{k}", [P, CT * IR], F32R) for k in range(3)]]
        w_lo = [keep["w_lo"][0], [sb(f"w_lo1_{k}", [P, CT * IR], F32R) for k in range(3)]]
        xt = sb("xt", [P, CT, TILE])
        xrow = sb("xrow", [P, 3, C])
        t_hi = [sb(f"t_hi{n}", [P, CT, TILE], F32R) for n in range(2)]
        t_lo = [sb(f"t_lo{n}", [P, CT, TILE], F32R) for n in range(2)]
        hid = [sb(f"hid{n}", [P, TILE]) for n in range(4)]
        h_hi = [sb(f"h_hi{n}", [P, TILE], F32R) for n in range(4)]
        h_lo = [sb(f"h_lo{n}", [P, TILE], F32R) for n in range(4)]
        ys = [sb(f"ys{n}", [P, TT, C]) for n in range(2)]
        x1 = sb("x1", [P, TT, C])
        picked = flat(raw[1][0]).rearrange("p (k t c) -> p k t c", k=2, t=TT)
        pick_no = sb("pick_no", [P, 2, TT], U32)
        pick_w = sb("pick_w", [P, 2, TT])

        gate = [psum(f"gate{n}", SEQ) for n in range(2)]
        up = [psum(f"up{n}", SEQ) for n in range(2)]
        y_ps = [psum(f"y_ps{n}", 2 * SEQ) for n in range(2)]

        raw_loaded, w_hi_done, w_split = keep["raw_loaded"], keep["w_hi_done"], keep["w_split"]
        tile_loaded = sem("tile_loaded")
        tile_t = sem("tile_t")
        tile_hi = sem("tile_hi")
        tile_split = sem("tile_split")
        gate_up_ready = sem("gate_up_ready")
        silu_done = sem("silu_done")
        hid_done = sem("hid_done")
        hid_hi = sem("hid_hi")
        hid_split = sem("hid_split")
        hid_used = sem("hid_used")
        y_read = sem("y_read")
        y_done = sem("y_done")
        y_stored = sem("y_stored")
        x1_loaded = sem("x1_loaded")
        picks_copied = sem("picks_copied")
        picked_rows = sem("picked_rows")
        sum_steps = sem("sum_steps")
        SUM_STEPS = 2 * TT - 1

        x1v = x1_dram.rearrange("(b t p) c -> b p t c", p=P, t=TT)
        outv = out.rearrange("b (t p) c -> b p t c", p=P)
        x2tv = x2t_dram.rearrange("(c p) t -> p c t", p=P)

        block = ctx.enter_context(nc.Block())

        @block.sync
        def _(sp):
            sgv, suv = (w.rearrange("(c p) n -> p c n", p=P) for w in (sg, su))
            sdv = sd.rearrange("(f p) n -> p f n", p=P)
            expert_w = (rg.rearrange("e (c p) n -> e p c n", p=P), ru.rearrange("e (c p) n -> e p c n", p=P),
                        rd.rearrange("e (f p) n -> e p f n", p=P))

            def load_weights(job, parity):
                sp.wait_ge(w_split, count(sp, PARTS * (job - 1)))
                if isinstance(job, int) and job == 1 + NE:
                    srcs = (sgv[:, :, IR:], suv[:, :, IR:], sdv[:, FT:, :])
                else:
                    srcs = tuple(one_batch(v, job - 1) for v in expert_w)
                for dst, src in zip(raw[parity], srcs):
                    sp.dma_start(dst[:], src).then_inc(raw_loaded, DMA)

            def slot_rows(t, table):
                first = CAP * t.index + SPLIT[0] * t.half
                return table[bass.ds(first, t.cols), :].rearrange("(t p) c -> p t c", p=P)

            def load_tile(t):
                sp.wait_ge(tile_split, count(sp, CT * t.no))
                if t.kind == "expert":
                    sp.dma_start(xrow[:, 0:t.rows, :], slot_rows(t, slots_dram)).then_inc(tile_loaded, DMA)
                else:
                    sp.dma_start(xt[:], x2tv[:, :, bass.ds(t.index * TILE, TILE)]).then_inc(tile_loaded, DMA)

            def store_tile(t, parity):
                sp.wait_ge(y_done, count(sp, t.no + 1))
                if t.kind == "first":
                    sp.dma_start(one_batch(x1v, t.index), ys[parity][:]).then_inc(y_stored, DMA)
                elif t.kind == "expert":
                    sp.dma_start(slot_rows(t, rows_dram), ys[parity][:, 0:t.rows, :]).then_inc(y_stored, DMA)
                else:
                    sp.dma_start(one_batch(outv, t.index), ys[parity][:]).then_inc(y_stored, DMA)

            def tile(before, t, after, parity, pieces, job):
                if t.kind == "expert" and t.half == 0 and not (isinstance(t.index, int) and t.index + 3 > 1 + NE):
                    load_weights(t.index + 3, t.set)
                if after:
                    load_tile(after)
                if before:
                    store_tile(before, 1 - parity)
                if t.kind != "expert":
                    if not before or before.kind == "expert":
                        sp.wait_ge(y_stored, count(sp, DMA * t.no))
                    sp.wait_ge(y_done, count(sp, t.no))
                    sp.dma_start(x1[:], one_batch(x1v, t.index)).then_inc(x1_loaded, DMA)

            load_tile(Tile("first", 0))
            load_weights(1, 1)
            load_weights(2, 0)
            all_tiles(sp, tile)
            store_tile(Tile("last", NB - 1), 1)
            sp.wait_ge(y_stored, DMA * END)

        @block.gpsimd
        def _(pool):
            with pool.Fori(0, NB) as n:
                stored, used = counts(pool, DMA * Z0, Z0 + n)
                pool.wait_ge(y_stored, stored)
                pool.wait_ge(y_done, used)
                pool.tensor_copy(pick_no[:], keep["row_no"][:, bass.ds(n, 1), :, :].rearrange("p n k t -> p (n k) t")
                                 ).then_inc(picks_copied, 1)
                pool.tensor_copy(pick_w[:], keep["choice_w"][:, bass.ds(n, 1), :, :].rearrange("p n k t -> p (n k) t")
                                 ).then_inc(picks_copied, 1)
                stored, copied = counts(pool, DMA * Z0, 2 * n + 2)
                pool.wait_ge(y_stored, stored)
                pool.wait_ge(picks_copied, copied)
                for t in range(TT):
                    for k in range(2):
                        pool.indirect_dma_start(
                            picked[:, k, t, :], None, rows_dram,
                            bass.IndirectOffsetOnAxis(ap=pick_no[:, k, t:t + 1], axis=0),
                            bounds_check=SLOTS, oob_is_err=False).then_inc(picked_rows, DMA)
            pool.wait_ge(picked_rows, DMA * 2 * TT * NB)

        @block.scalar
        def _(act):
            def tile_hi_part(t, parity):
                for c in range(CT):
                    if t.kind == "expert":
                        act.wait_ge(tile_t, count(act, CT * (t.no - E0) + c + 1))
                        src = y_ps[parity][:, SEQ * c:SEQ * c + t.cols]
                    else:
                        act.wait_ge(tile_loaded, count(act, DMA * (t.no + 1)))
                        src = xt[:, c, :]
                    act.activation(t_hi[parity][:, c, 0:t.cols], src, ACT.Copy).then_inc(tile_hi, 1)

            def tile(before, t, after, parity, pieces, job):
                per_step = len(pieces) // FT
                for f in range(FT):
                    no = FT * t.no + f
                    ready, split = counts(act, no + 1, no - 3)
                    act.wait_ge(gate_up_ready, ready)
                    act.wait_ge(hid_split, split)
                    act.activation(hid[f % 4][:, 0:t.cols], gate[f % 2][:, 0:t.cols], ACT.Silu).then_inc(silu_done, 1)
                    for n in pieces[per_step * f:per_step * (f + 1)]:
                        if n == 0:
                            act.wait_ge(raw_loaded, count(act, 3 * DMA * (job + 1)))
                        for k, cols in piece_parts(n):
                            act.activation(w_hi[1 - t.set][k][:, cols], flat(raw[1 - t.set][k])[:, cols],
                                           ACT.Copy).then_inc(w_hi_done, 1)
                    made, used = counts(act, no + 1, no - 3)
                    act.wait_ge(hid_done, made)
                    act.wait_ge(hid_used, used)
                    act.activation(h_hi[f % 4][:, 0:t.cols], hid[f % 4][:, 0:t.cols], ACT.Copy).then_inc(hid_hi, 1)
                    if f == 5 and after:
                        tile_hi_part(after, 1 - parity)

            tile_hi_part(Tile("first", 0), 0)
            all_tiles(act, tile)

        @block.vector
        def _(dve):
            def tile_lo_part(t, parity):
                for c in range(CT):
                    dve.wait_ge(tile_hi, count(dve, CT * t.no + c + 1))
                    src = y_ps[parity][:, SEQ * c:SEQ * c + t.cols] if t.kind == "expert" else xt[:, c, :]
                    dve.tensor_tensor(t_lo[parity][:, c, 0:t.cols], src, t_hi[parity][:, c, 0:t.cols].bitcast(F32),
                                      ALU.subtract).then_inc(tile_split, 1)

            def finish(t, parity):
                y = y_ps[parity][:, 0:C * t.rows].rearrange("p (t c) -> p t c", c=C)
                summed, stored = counts(dve, FT * (t.no + 1), DMA * (t.no - 1))
                dve.wait_ge(hid_used, summed)
                dve.wait_ge(y_stored, stored)
                if t.kind == "expert":
                    dve.tensor_copy(ys[parity][:, 0:t.rows, :], y).then_inc(y_done, 1)
                elif t.kind == "first":
                    dve.wait_ge(x1_loaded, count(dve, DMA * (t.index + 1)))
                    dve.tensor_tensor(ys[parity][:], y, x1[:], ALU.add).then_inc(y_done, 1)
                else:
                    dve.wait_ge(x1_loaded, count(dve, DMA * (NB + t.index + 1)))
                    dve.tensor_tensor(ys[parity][:], y, x1[:], ALU.add).then_inc(y_read, 1)
                    added, there = counts(dve, t.index + 1, DMA * 2 * TT * (t.index + 1))
                    dve.wait_ge(y_read, added)
                    dve.wait_ge(picked_rows, there)
                    for k in range(2):
                        for r in range(TT):
                            ins = dve.scalar_tensor_tensor(out=ys[parity][:, r, :], in0=picked[:, k, r, :],
                                                           scalar=pick_w[:, k, r:r + 1], in1=ys[parity][:, r, :],
                                                           op0=ALU.mult, op1=ALU.add)
                            if k == 1 and r == TT - 1:
                                ins.then_inc(y_done, 1)
                            else:
                                ins.then_inc(sum_steps, 1)
                        if k == 0:
                            dve.wait_ge(sum_steps, count(dve, SUM_STEPS * t.index + TT))

            def tile(before, t, after, parity, pieces, job):
                per_step = len(pieces) // FT
                for f in range(FT):
                    no = FT * t.no + f
                    dve.wait_ge(silu_done, count(dve, no + 1))
                    dve.tensor_tensor(hid[f % 4][:, 0:t.cols], up[f % 2][:, 0:t.cols], hid[f % 4][:, 0:t.cols],
                                      ALU.mult).then_inc(hid_done, 1)
                    for n in pieces[per_step * f:per_step * (f + 1)]:
                        for m, (k, cols) in enumerate(piece_parts(n)):
                            dve.wait_ge(w_hi_done, count(dve, PARTS * job + PARTS_BEFORE[n] + m + 1))
                            dve.tensor_tensor(w_lo[1 - t.set][k][:, cols], flat(raw[1 - t.set][k])[:, cols],
                                              w_hi[1 - t.set][k][:, cols].bitcast(F32), ALU.subtract).then_inc(w_split, 1)
                    dve.wait_ge(hid_hi, count(dve, no + 1))
                    dve.tensor_tensor(h_lo[f % 4][:, 0:t.cols], hid[f % 4][:, 0:t.cols],
                                      h_hi[f % 4][:, 0:t.cols].bitcast(F32), ALU.subtract).then_inc(hid_split, 1)
                    if f == 2 and before:
                        finish(before, 1 - parity)
                    if f == 5 and after:
                        tile_lo_part(after, 1 - parity)

            tile_lo_part(Tile("first", 0), 0)
            all_tiles(dve, tile)
            finish(Tile("last", NB - 1), 1)

        @block.tensor
        def _(pe):
            def transposes(t, parity):
                loaded, left = counts(pe, DMA * (t.no + 1), t.no - 1)
                pe.wait_ge(tile_loaded, loaded)
                pe.wait_ge(y_done, left)
                for c in range(CT):
                    for r in range(t.rows):
                        ins = pe.transpose(y_ps[parity][:, SEQ * c + P * r:SEQ * c + P * r + P],
                                           xrow[:, r, P * c:P * c + P], ident[:])
                    ins.then_inc(tile_t, 1)

            def gate_up(t, parity, f):
                no = FT * t.no + f
                if f == 0:
                    tile_there, w_there = counts(pe, CT * (t.no + 1), PARTS * (t.job + 1))
                    pe.wait_ge(tile_split, tile_there)
                    pe.wait_ge(w_split, w_there)
                pe.wait_ge(hid_done, count(pe, no - 1))
                for k, ps in ((0, gate[f % 2]), (1, up[f % 2])):
                    hi, lo = (w[t.set][k][:].rearrange("p (c n) -> p c n", c=CT) for w in (w_hi, w_lo))
                    cols = slice(P * f, P * f + P)
                    parts = [(w[:, c, cols], xp[parity][:, c, 0:t.cols]) for c in range(CT)
                             for w, xp in ((hi, t_hi), (hi, t_lo), (lo, t_hi))]
                    for m, (w, xp) in enumerate(parts):
                        ins = pe.matmul(ps[:, 0:t.cols], w, xp, start=(m == 0), stop=(m == len(parts) - 1))
                ins.then_inc(gate_up_ready, 1)

            def down(t, parity, f):
                no = FT * t.no + f
                split, left = counts(pe, no + 1, t.no - 1)
                pe.wait_ge(hid_split, split)
                if f == 0:
                    pe.wait_ge(y_done, left)
                hi, lo = (w[t.set][2][:, C * f:C * f + C] for w in (w_hi, w_lo))
                for r in range(t.rows):
                    rows = slice(P * r, P * r + P)
                    parts = ((h_hi[f % 4][:, rows], hi), (h_hi[f % 4][:, rows], lo), (h_lo[f % 4][:, rows], hi))
                    for m, (h, w) in enumerate(parts):
                        ins = pe.matmul(y_ps[parity][:, C * r:C * r + C], h, w,
                                        start=(f == 0 and m == 0 and r % 2 == 0),
                                        stop=(f == FT - 1 and m == 2), skip_group_check=True)
                ins.then_inc(hid_used, 1)

            def tile(before, t, after, parity, pieces, job):
                for f in range(FT):
                    gate_up(t, parity, f)
                    if f >= 2:
                        down(t, parity, f - 2)
                    elif before:
                        down(before, 1 - parity, FT - 2 + f)
                    if f == 4 and after and after.kind == "expert":
                        transposes(after, 1 - parity)

            all_tiles(pe, tile)
            for f in (FT - 2, FT - 1):
                down(Tile("last", NB - 1), 1, f)


def program(nc, x, w_qkv, b_qkv, w_proj, b_proj, router_w, rg, ru, rd, sg, su, sd, out):
    x1_dram = nc.dram_tensor("x1_rows", [TOKENS, C], F32, kind="Internal").ap()
    x2t_dram = nc.dram_tensor("x2_transposed", [C, TOKENS], F32, kind="Internal").ap()
    slots_dram = nc.dram_tensor("slots", [SLOTS, C], F32, kind="Internal").ap()
    rows_dram = nc.dram_tensor("expert_rows", [SLOTS + 1, C], F32, kind="Internal").ap()
    recip_dram = nc.dram_tensor("recips", [2, GRP, SEQ], F32, kind="Internal").ap()
    with ExitStack() as ctx:
        def sb(name, shape, dt=F32):
            return ctx.enter_context(nc.sbuf_tensor(name, shape, dt))

        keep = {
            "ident": sb("ident", [P, P]),
            "row_no": sb("kept_row_no", [P, NB, 2, TT], U32),
            "choice_w": sb("kept_choice_w", [P, NB, 2, TT]),
            "raw": [[sb("raw0_g", [P, CT, IR]), sb("raw0_u", [P, CT, IR]), sb("raw0_d", [P, FT, C])]],
            "w_hi": [[sb(f"w_hi0_{k}", [P, CT * IR], F32R) for k in range(3)]],
            "w_lo": [[sb(f"w_lo0_{k}", [P, CT * IR], F32R) for k in range(3)]],
        }
        for name in ("raw_loaded", "w_hi_done", "w_split"):
            keep[name] = ctx.enter_context(nc.semaphore(name))
        attention_block(nc, x, w_qkv, b_qkv, w_proj, b_proj, router_w, sg, su, sd,
                        x1_dram, x2t_dram, slots_dram, rows_dram, recip_dram, keep)
        ffn_block(nc, sg, su, sd, rg, ru, rd, x1_dram, x2t_dram, slots_dram, rows_dram, keep, out)


_INS = ["L0_attn_x", "L0_attn_w_qkv", "L0_attn_b_qkv", "L0_attn_w_proj", "L0_attn_b_proj", "L0_ffn_router_w",
        "L0_ffn_rg", "L0_ffn_ru", "L0_ffn_rd", "L0_ffn_sg", "L0_ffn_su", "L0_ffn_sd"]


def kernel(**inputs):
    import numpy as np
    import concourse.bacc as bacc
    from concourse.bass_utils import run_bass_kernel_spmd

    nc = bacc.Bacc("TRN2", target_bir_lowering=False, num_devices=1)
    arrays, args = {}, []
    for name in _INS:
        a = np.ascontiguousarray(inputs[name])
        arrays[f"in_{name}"] = a
        args.append(nc.dram_tensor(f"in_{name}", a.shape, mybir.dt.from_np(a.dtype), kind="ExternalInput").ap())
    args.append(nc.dram_tensor("block_out", (NB, SEQ, C), F32, kind="ExternalOutput").ap())
    program(nc, *args)
    r = run_bass_kernel_spmd(nc, [arrays], core_ids=[0])
    return r.results[0]["block_out"]
```

```python
from contextlib import ExitStack

import concourse.bass as bass
from concourse import mybir

F32 = mybir.dt.float32
F32R = mybir.dt.float32r
BF16 = mybir.dt.bfloat16
U32 = mybir.dt.uint32
ALU = mybir.AluOpType
ACT = mybir.ActivationFunctionType
AX = mybir.AxisListType

P = 128
NB, SEQ, C = 8, 512, 256
NH, HD = 16, 16
CT = C // P
TT = SEQ // P
KT = SEQ // P
GRP = 4
NG = NH // GRP
PAIRS = NH // 2
NE, IR = 8, 4 * C
TOKENS = NB * SEQ
CAP = int(1.25 * TOKENS / NE)
SLOTS = NE * CAP
LN_EPS = 1e-5
RMS_EPS = 1.1920928955078125e-07
SCALE = HD ** -0.5
ROWS_MAX = 65
ROWS_EXP = ROWS_MAX + 2
FT = IR // P
XT_SLOTS, QK_SLOTS, V_SLOTS, PROJ_SLOTS = (0, 2), (3, 5, 13, 15), (4, 9), (7, 8)
ZERO_STORES = SLOTS // P // 4 + 1
DMA = 16

PIECES = 2 * FT
PIECE = 3 * CT * IR // PIECES


def piece_parts(n):
    parts, at, end = [], n * PIECE, (n + 1) * PIECE
    while at < end:
        k, off = divmod(at, CT * IR)
        m = min(end - at, CT * IR - off)
        parts.append((k, slice(off, off + m)))
        at += m
    return parts


PARTS_BEFORE = [sum(len(piece_parts(m)) for m in range(n)) for n in range(PIECES + 1)]
PARTS = PARTS_BEFORE[PIECES]


def count(eng, value):
    return max(value, 0) if isinstance(value, int) else eng.to_reg(value)


def counts(eng, *values):
    return [count(eng, v) for v in values]


def flat(tensor):
    return tensor[:].rearrange("p a b -> p (a b)")


def one_batch(view, n):
    return view[n] if isinstance(n, int) else view[bass.ds(n, 1)].rearrange("b p t c -> (b p) t c")


def send_rows(pool, slots_dram, keep):
    for t in range(TT):
        for k in range(2):
            pool.indirect_dma_start(
                slots_dram, bass.IndirectOffsetOnAxis(ap=keep["sent_row_no"][:, k, t:t + 1], axis=0),
                keep["xn2"][:, t, :], None, bounds_check=SLOTS - 1, oob_is_err=False).then_inc(keep["rows_sent"], DMA)


class Reader:

    def __init__(self):
        self.sem, self.value = None, 0

    def is_(self, sem, value):
        self.sem, self.value = sem, value


def attention_block(nc, x, w_qkv, b_qkv, w_proj, b_proj, router_w, sg, su, sd,
                    x1_dram, x2t_dram, slots_dram, rows_dram, recip_dram, keep):
    with ExitStack() as ctx:
        def sb(name, shape, dt=F32):
            return ctx.enter_context(nc.sbuf_tensor(name, shape, dt))

        def psum(name, cols):
            return ctx.enter_context(nc.psum_tensor(name, [P, cols], F32))

        def sem(name):
            return ctx.enter_context(nc.semaphore(name))

        ident = keep["ident"]
        before = sb("before", [P, P], BF16)
        ones = sb("ones", [P, P], BF16)
        expert_no = sb("expert_no", [P, TT, NE])
        rank = sb("rank", [P, TT, NE])
        minus_half = sb("minus_half", [P, TT])
        zeros = keep["raw"][0][1][:, 1, :]
        wq_raw = flat(keep["raw"][0][2])[:, 0:CT * 3 * C].rearrange("p (c n) -> p c n", c=CT)
        xs = keep["raw"][0][0][:, 0, :].rearrange("p (t c) -> p t c", t=TT)
        xn = keep["raw"][0][0][:, 1, :].rearrange("p (t c) -> p t c", t=TT)
        v_new = keep["raw"][0][1][:, 0, :].rearrange("p (t c) -> p t c", t=KT)
        q_st = keep["w_hi"][0][0][:].rearrange("p (h n) -> p h n", n=SEQ), keep["w_hi"][0][1][:].rearrange("p (h n) -> p h n", n=SEQ)
        k_st = keep["w_lo"][0][0][:].rearrange("p (h n) -> p h n", n=SEQ), keep["w_lo"][0][1][:].rearrange("p (h n) -> p h n", n=SEQ)
        qk_hi = keep["w_hi"][0][2][:].rearrange("p (m n) -> p m n", n=SEQ)
        qk_lo = keep["w_lo"][0][2][:].rearrange("p (m n) -> p m n", n=SEQ)
        wq_hi = sb("wq_hi", [P, CT, 3 * C], F32R)
        wq_lo = sb("wq_lo", [P, CT, 3 * C], F32R)
        wp = sb("wp", [P, NG, C])
        rw_raw = sb("rw_raw", [NE, C])
        rwt = sb("rwt", [P, CT, 32])
        bias_qk = sb("bias_qk", [P, 4])
        bias_v = sb("bias_v", [P, 1, C])
        st1 = sb("st1", [P, TT, 6])
        mv1 = sb("mv1", [P, TT, 2])
        rstd1 = sb("rstd1", [P, TT])
        xt_hi = sb("xt_hi", [P, CT, SEQ], F32R)
        xt_lo = sb("xt_lo", [P, CT, SEQ], F32R)
        v_aug = sb("v_aug", [P, KT, NH, 2 * HD])
        qk_raw = sb("qk_raw", [P, 2, SEQ])
        mx = sb("mx", [P, 2, 2 * TT])
        mt_hi = sb("mt_hi", [2 * TT, 2, P], F32R)
        mt_lo = sb("mt_lo", [2 * TT, 2, P], F32R)
        probs = sb("probs", [P, 2, GRP, KT, SEQ])
        o_sb = sb("o_sb", [P, 2, SEQ])
        den = sb("den", [P, HD])
        rden = sb("rden", [P, HD])
        r_wide = sb("r_wide", [P, SEQ])
        heads = sb("heads", [P, NG, SEQ])
        xr = sb("xr", [P, TT, C])
        st2 = sb("st2", [P, TT, 6])
        mv2 = sb("mv2", [P, TT, 2])
        rstd2 = sb("rstd2", [P, TT])
        xn2, row_no, rows_sent = keep["xn2"], keep["sent_row_no"], keep["rows_sent"]
        sq = sb("sq", [P, C])
        ssq = sb("ssq", [P, TT])
        ms = sb("ms", [P, TT])
        rrms = sb("rrms", [P, TT])
        x2t = sb("x2t", [P, CT, SEQ])
        lgt = sb("lgt", [P, P])
        lg = sb("lg", [P, TT, NE])
        top = sb("top", [P, 2, TT])
        gap = sb("gap", [P, 2, TT])
        best = sb("best", [P, TT])
        key = sb("key", [P, TT, NE])
        chosen = sb("chosen", [P, 2, TT * NE])
        mask = sb("mask", [P, TT * NE], BF16)
        base = sb("base", [P, NE])
        pos = sb("pos", [P, TT, NE])
        slot_all = sb("slot_all", [P, TT, NE])
        picks = sb("picks", [P, 2, TT * NE])
        place = sb("place", [P, 2, TT])
        slot = sb("slot", [P, 2, TT])
        share = sb("share", [P, 2, TT])
        total = sb("total", [P, TT])

        s_max = [psum(f"s_max{n}", SEQ) for n in range(TT)]
        s_exp = [psum(f"s_exp{n}", SEQ) for n in range(2)]
        o_ps = psum("o_ps", SEQ)
        m_ps = psum("m_ps", SEQ)

        consts_made = sem("consts_made")
        dve_consts = sem("dve_consts")
        wq_loaded = sem("wq_loaded")
        bias_loaded = sem("bias_loaded")
        rw_loaded = sem("rw_loaded")
        rwt_ready = sem("rwt_ready")
        rwt_copied = sem("rwt_copied")
        wq_hi_done = sem("wq_hi_done")
        wq_lo_done = sem("wq_lo_done")
        wp_zeroed = sem("wp_zeroed")
        wp_loaded = sem("wp_loaded")
        rows_zeroed = sem("rows_zeroed")
        x_loaded = sem("x_loaded")
        xr_loaded = sem("xr_loaded")
        ln1_steps = sem("ln1_steps")
        ln1_stats = sem("ln1_stats")
        ln1_rstd = sem("ln1_rstd")
        ln1_done = sem("ln1_done")
        xt_ready = sem("xt_ready")
        xt_hi_done = sem("xt_hi_done")
        xt_split = sem("xt_split")
        qk_ready = sem("qk_ready")
        qk_read = sem("qk_read")
        qk_hi_done = sem("qk_hi_done")
        qk_split = sem("qk_split")
        v_ready = sem("v_ready")
        v_there = sem("v_there")
        v_copied = sem("v_copied")
        pair_loaded = [sem(f"pair_loaded{n}") for n in range(2)]
        s_max_ready = sem("s_max_ready")
        max_done = sem("max_done")
        mt_ready = sem("mt_ready")
        mt_hi_done = sem("mt_hi_done")
        mt_split = sem("mt_split")
        max_loaded = [sem(f"max_loaded{n}") for n in range(2)]
        s_exp_ready = sem("s_exp_ready")
        exp_done = sem("exp_done")
        pv_done = sem("pv_done")
        o_copied = sem("o_copied")
        den_loaded = sem("den_loaded")
        den_inverted = sem("den_inverted")
        recip_stored = sem("recip_stored")
        recip_loaded = sem("recip_loaded")
        heads_done = sem("heads_done")
        proj_ready = sem("proj_ready")
        x1_done = sem("x1_done")
        x1_stored = sem("x1_stored")
        ln2_steps = sem("ln2_steps")
        ln2_stats = sem("ln2_stats")
        ln2_rstd = sem("ln2_rstd")
        ln2_done = sem("ln2_done")
        ssq_done = sem("ssq_done")
        ms_done = sem("ms_done")
        rms_done = sem("rms_done")
        x2t_ready = sem("x2t_ready")
        x2t_copied = sem("x2t_copied")
        x2t_stored = sem("x2t_stored")
        logits_ready = sem("logits_ready")
        lgt_copied = sem("lgt_copied")
        lg_ready = sem("lg_ready")
        logits_read = sem("logits_read")
        choice_steps = sem("choice_steps")
        gap_known = sem("gap_known")
        gap_exp_done = sem("gap_exp_done")
        mask_done = sem("mask_done")
        pos_ready = sem("pos_ready")
        pos_read = sem("pos_read")
        slot_steps = sem("slot_steps")
        rows_known = sem("rows_known")

        xv = x.rearrange("b (t p) c -> b p t c", p=P)
        x1v = x1_dram.rearrange("(b t p) c -> b p t c", p=P, t=TT)
        x2tv = x2t_dram.rearrange("(c p) t -> p c t", p=P)

        block = ctx.enter_context(nc.Block())

        @block.sync
        def _(sp):
            sp.dma_start(xs, xv[0]).then_inc(x_loaded, DMA)
            sp.dma_start(wq_raw, w_qkv.rearrange("(c p) n -> p c n", p=P)).then_inc(wq_loaded, DMA)
            for m in range(4):
                first = (m % 2) * C + (m // 2) * P
                for j in range(2):
                    sp.dma_start(bias_qk[j:P:2, m:m + 1],
                                 b_qkv[first:first + P].rearrange("(r j d a) -> j r d a", j=2, d=HD, a=1)[j]
                                 ).then_inc(bias_loaded, DMA)
            sp.dma_start(bias_v[:, 0, :], b_qkv[2 * C:3 * C].partition_broadcast(P)).then_inc(bias_loaded, DMA)
            sp.dma_start(rw_raw[:], router_w).then_inc(rw_loaded, DMA)
            sp.wait_ge(wp_zeroed, 1)
            wpv = w_proj.rearrange("(g j d) n -> j d g n", g=NG, j=GRP)
            for j in range(GRP):
                sp.dma_start(wp[32 * j:32 * j + HD, :, :], wpv[j]).then_inc(wp_loaded, DMA)
            sp.dma_start(wp[HD:HD + 1, 0, :], b_proj.rearrange("(a n) -> a n", a=1)).then_inc(wp_loaded, DMA)

            def load_pair(i, c, which):
                n, cc = i + c // PAIRS, c % PAIRS
                tile, row, half, ring = cc // 4, 32 * (cc % 4), (c % 4) // 2, 2 * (c % 2)
                if which == 0:
                    tile_split, old_waited, old_used = counts(
                        sp, 4 * n + 2 * (tile + 1), 8 * (PAIRS * i + c) - 15, 8 * (PAIRS * i + c) - 24)
                    sp.wait_ge(qk_split, tile_split)
                    sp.wait_ge(s_max_ready, old_waited)
                    sp.wait_ge(s_exp_ready, old_used)
                    copies = (q_st, 0, qk_hi), (q_st, 1, qk_hi), (q_st, 2, qk_lo), (k_st, 0, qk_hi)
                else:
                    copies = (k_st, 1, qk_lo), (k_st, 2, qk_hi)
                for to, r, part in copies:
                    sp.dma_start(to[half][HD * r:HD * r + HD, ring:ring + 2, :].bitcast(F32),
                                 part[row:row + 32, 2 * tile + (to is k_st), :].bitcast(F32)
                                 ).then_inc(pair_loaded[c % 2], DMA)

            def load_max(i, c):
                half, ring = (c % 4) // 2, 2 * (c % 2)
                sp.wait_ge(mt_split, count(sp, PAIRS * i + c + 1))
                for r, part in enumerate((mt_hi, mt_lo)):
                    row = ROWS_MAX + r
                    sp.dma_start(q_st[half][row:row + 1, ring:ring + 2, :].bitcast(F32),
                                 part[:, c % 2, :].bitcast(F32)).then_inc(max_loaded[c % 2], DMA)

            def store_recip(i, g):
                sp.wait_ge(den_inverted, count(sp, NG * i + g + 1))
                sp.dma_start(recip_dram[g % 2].rearrange("j (a n) -> (j a) n", n=HD), rden[:]).then_inc(recip_stored, DMA)

            def load_recip(i, g):
                stored, used = counts(sp, DMA * (NG * i + g + 1), NG * i + g)
                sp.wait_ge(recip_stored, stored)
                sp.wait_ge(heads_done, used)
                sp.dma_start(r_wide[:], recip_dram[g % 2].rearrange("j (a n) -> j a n", a=1).to_broadcast([GRP, 32, SEQ])
                             ).then_inc(recip_loaded, DMA)

            def store_x1(n):
                sp.wait_ge(x1_done, count(sp, 2 * n + 2))
                sp.dma_start(one_batch(x1v, n), xr[:]).then_inc(x1_stored, DMA)

            def load_xr(n):
                read, stored = counts(sp, n, DMA * n)
                sp.wait_ge(ln2_done, read)
                sp.wait_ge(x1_stored, stored)
                sp.dma_start(xr[:], one_batch(xv, n)).then_inc(xr_loaded, DMA)

            def store_x2t(n):
                sp.wait_ge(x2t_copied, count(sp, CT * (n + 1)))
                sp.dma_start(x2tv[:, :, bass.ds(n * SEQ, SEQ)], x2t[:]).then_inc(x2t_stored, DMA)

            def load_x(n):
                sp.wait_ge(ln1_done, count(sp, n))
                sp.dma_start(xs, one_batch(xv, n)).then_inc(x_loaded, DMA)

            def load_ffn_weights(k):
                sp.wait_ge(v_copied, NG * NB)
                sp.wait_ge(xt_ready, CT * NB)
                sp.wait_ge(rows_zeroed, DMA * ZERO_STORES)
                src = (sg.rearrange("(c p) n -> p c n", p=P)[:, :, 0:IR], su.rearrange("(c p) n -> p c n", p=P)[:, :, 0:IR],
                       sd.rearrange("(f p) n -> p f n", p=P)[:, 0:FT, :])[k]
                sp.dma_start(keep["raw"][0][k][:], src).then_inc(keep["raw_loaded"], DMA)

            def body(i, first, last, more_x):
                for s in range(NH):
                    g, j = s // GRP, s % GRP
                    if last and s in (9, 11, 13):
                        load_ffn_weights(s // 2 - 4)
                    if j == 1 and (not first or g >= 2):
                        store_recip(i, g - 2)
                    recip_follows = j == 2 and (not first or g >= 2)
                    if recip_follows and g == 1:
                        load_recip(i, g - 2)
                    pair_follows = s % 2 == 0 and not (last and s // 2 + 3 >= PAIRS)
                    if pair_follows:
                        load_pair(i, s // 2 + 3, 0)
                    if recip_follows and g != 1:
                        load_recip(i, g - 2)
                    if s % 2 == 0 and not (last and s == 14):
                        load_max(i, s // 2 + 1)
                    if pair_follows:
                        load_pair(i, s // 2 + 3, 1)
                    if s == 0 and more_x:
                        load_x(i + 2)
                    if s == 10 and not first:
                        store_x1(i - 1)
                    if s == 12 and not first:
                        store_x2t(i - 1)
                    if s == 14:
                        load_xr(i)

            load_x(1)
            sp.wait_ge(dve_consts, 7)
            for c in range(3):
                load_pair(0, c, 0)
                load_pair(0, c, 1)
            load_max(0, 0)
            body(0, True, False, True)
            with sp.Fori(1, NB - 2) as i:
                body(i, False, False, True)
            body(NB - 2, False, False, False)
            body(NB - 1, False, True, False)
            for g in (2, 3):
                store_recip(NB - 1, g)
                load_recip(NB - 1, g)
            store_x1(NB - 1)
            store_x2t(NB - 1)
            sp.wait_ge(x1_stored, DMA * NB)
            sp.wait_ge(x2t_stored, DMA * NB)

        @block.gpsimd
        def _(pool):
            pool.memset(ident[:], 0.0).then_inc(consts_made, 1)
            pool.memset(before[:], 0.0).then_inc(consts_made, 1)
            pool.memset(zeros, 0.0).then_inc(consts_made, 1)
            pool.memset(ones[:], 1.0).then_inc(consts_made, 1)
            pool.memset(minus_half[:], -0.5).then_inc(consts_made, 1)
            pool.iota(expert_no[:], pattern=[[0, TT], [1, NE]], base=0, channel_multiplier=0,
                      allow_small_or_imprecise_dtypes=True).then_inc(consts_made, 1)
            pool.iota(rank[:], pattern=[[0, TT], [-1, NE]], base=NE, channel_multiplier=0,
                      allow_small_or_imprecise_dtypes=True).then_inc(consts_made, 1)
            pool.wait_ge(consts_made, 7)
            pool.affine_select(out=ident[:], in_=ident[:], compare_op=ALU.not_equal, fill=1.0, base=0,
                               pattern=[[-1, P]], channel_multiplier=1).then_inc(consts_made, 1)
            pool.affine_select(out=before[:], in_=before[:], compare_op=ALU.is_ge, fill=1.0, base=0,
                               pattern=[[-1, P]], channel_multiplier=1).then_inc(consts_made, 1)
            zv = slots_dram.rearrange("(n p r) c -> n p (r c)", p=P, r=4)
            for n in range(ZERO_STORES - 1):
                pool.dma_start(zv[n], zeros).then_inc(rows_zeroed, DMA)
            pool.dma_start(rows_dram[SLOTS:SLOTS + 1, :], zeros[0:1, 0:C]).then_inc(rows_zeroed, DMA)

            def qk_lo_part(n, m):
                pool.wait_ge(qk_hi_done, count(pool, 4 * n + m + 1))
                pool.tensor_tensor(qk_lo[:, m, :], qk_raw[:, m % 2, :], qk_hi[:, m, :].bitcast(F32),
                                   ALU.subtract).then_inc(qk_split, 1)

            def v_copy(n, g):
                there, used = counts(pool, 2 * n + 2, NG * n + g - 3)
                pool.wait_ge(v_there, there)
                pool.wait_ge(pv_done, used)
                cols = slice(GRP * HD * g, GRP * HD * (g + 1))
                pool.tensor_tensor(v_aug[:, :, GRP * g:GRP * g + GRP, 0:HD],
                                   v_new[:, :, cols].rearrange("p t (h d) -> p t h d", h=GRP),
                                   bias_v[:, :, cols].rearrange("p t (h d) -> p t h d", h=GRP).to_broadcast(
                                       [P, KT, GRP, HD]),
                                   ALU.add).then_inc(v_copied, 1)

            def rstd1_of(n):
                pool.wait_ge(ln1_stats, count(pool, n + 1))
                pool.tensor_tensor(rstd1[:], mv1[:, :, 1], minus_half[:], ALU.pow).then_inc(ln1_rstd, 1)

            def rstd2_of(n):
                pool.wait_ge(ln2_stats, count(pool, n + 1))
                pool.tensor_tensor(rstd2[:], mv2[:, :, 1], minus_half[:], ALU.pow).then_inc(ln2_rstd, 1)

            def rms_of(n):
                made, summed = counts(pool, 9, TT * (n + 1))
                pool.wait_ge(consts_made, made)
                pool.wait_ge(ssq_done, summed)
                pool.tensor_scalar(ms[:], ssq[:], 1.0 / C, RMS_EPS, ALU.mult, ALU.add).then_inc(ms_done, 1)
                pool.wait_ge(ms_done, count(pool, n + 1))
                pool.tensor_tensor(rrms[:], ms[:], minus_half[:], ALU.pow).then_inc(rms_done, 1)

            def normalise_heads(i, g):
                loaded, projected = counts(pool, DMA * (NG * i + g + 1), 2 * (i + g // NG))
                pool.wait_ge(recip_loaded, loaded)
                pool.wait_ge(proj_ready, projected)
                pool.tensor_tensor(heads[:, g % NG, :], o_sb[:, g % 2, :], r_wide[:], ALU.mult).then_inc(heads_done, 1)

            def dispatch(n):
                if isinstance(n, int) and n == 0:
                    pool.wait_ge(rows_zeroed, DMA * ZERO_STORES)
                made, known = counts(pool, 9, n + 1)
                pool.wait_ge(consts_made, made)
                pool.wait_ge(rows_known, known)
                send_rows(pool, slots_dram, keep)

            def body(i, first, last, more_x):
                if not first:
                    for g in range(3):
                        v_copy(i, g)
                if not last:
                    qk_lo_part(i + 1, 0)
                if not first:
                    normalise_heads(i, -2)
                    v_copy(i, 3)
                if more_x:
                    rstd1_of(i + 2)
                if not last:
                    qk_lo_part(i + 1, 1)
                if not first:
                    normalise_heads(i, -1)
                    rstd2_of(i - 1)
                normalise_heads(i, 0)
                if not first:
                    rms_of(i - 1)
                if not last:
                    qk_lo_part(i + 1, 2)
                    qk_lo_part(i + 1, 3)
                normalise_heads(i, 1)
                if not first:
                    dispatch(i - 1)

            rstd1_of(0)
            pool.wait_ge(bias_loaded, DMA * 9)
            pool.wait_ge(dve_consts, 7)
            for m in range(4):
                qk_lo_part(0, m)
            for g in range(NG):
                v_copy(0, g)
            rstd1_of(1)
            body(0, True, False, True)
            body(1, False, False, True)
            with pool.Fori(2, NB - 2) as i:
                body(i, False, False, True)
            body(NB - 2, False, False, False)
            body(NB - 1, False, True, False)
            for g in (2, 3):
                normalise_heads(NB - 1, g)
            rstd2_of(NB - 1)
            rms_of(NB - 1)

        @block.scalar
        def _(act):
            act.wait_ge(wq_loaded, DMA)
            for c in range(CT):
                for part in range(2):
                    src = wq_raw[:, c, part * C:(part + 1) * C].rearrange("p (r j d) -> p r d j", j=2, d=HD)
                    dst = wq_hi[:, c, part * C:(part + 1) * C].rearrange("p (r d j) -> p r d j", j=2, d=HD)
                    act.activation(dst, src, ACT.Copy).then_inc(wq_hi_done, 1)
                act.activation(wq_hi[:, c, 2 * C:], wq_raw[:, c, 2 * C:], ACT.Copy).then_inc(wq_hi_done, 1)

            def xt_hi_part(n, c):
                act.wait_ge(xt_ready, count(act, CT * n + c + 1))
                act.activation(xt_hi[:, c, :], m_ps[:], ACT.Copy).then_inc(xt_hi_done, 1)

            def qk_read_part(n, m):
                ready, old = counts(act, 4 * n + m + 1, 4 * n + m - 1)
                act.wait_ge(qk_ready, ready)
                act.wait_ge(qk_split, old)
                act.activation(qk_raw[:, m % 2, :], m_ps[:], ACT.Identity, bias=bias_qk[:, m:m + 1]).then_inc(qk_read, 1)

            def qk_hi_part(n, m):
                there, left = counts(act, 4 * n + m + 1, 8 * (PAIRS * (n - 1) + 4 * (m // 2) + 3) + 1)
                act.wait_ge(qk_read, there)
                act.wait_ge(s_max_ready, left)
                act.activation(qk_hi[:, m, :], qk_raw[:, m % 2, :], ACT.Copy).then_inc(qk_hi_done, 1)

            def v_read(n, t):
                ready, copied = counts(act, 2 * n + t + 1, NG * n)
                act.wait_ge(v_ready, ready)
                act.wait_ge(v_copied, copied)
                act.activation(v_new[:, 2 * t:2 * t + 2, :], m_ps[:].rearrange("p (t c) -> p t c", t=2),
                               ACT.Copy).then_inc(v_there, 1)

            def mt_hi_part(i, c):
                ready, used = counts(act, PAIRS * i + c + 1, 8 * (PAIRS * i + c) - 15)
                act.wait_ge(mt_ready, ready)
                act.wait_ge(s_exp_ready, used)
                act.activation(mt_hi[:, c % 2, :], m_ps[0:2 * TT, 0:P], ACT.Copy).then_inc(mt_hi_done, 1)

            def exps(i, s, k):
                g = s // GRP
                ready, used = counts(act, KT * (NH * i + s) + k + 1, NG * i + g - 1)
                act.wait_ge(s_exp_ready, ready)
                act.wait_ge(pv_done, used)
                act.activation(probs[:, g % 2, s % GRP, k, :], s_exp[k % 2][:], ACT.Exp,
                               scale=SCALE).then_inc(exp_done, 1)

            def copy_o(i, g):
                ready, used = counts(act, NG * i + g + 1, NG * i + g - 1)
                act.wait_ge(pv_done, ready)
                act.wait_ge(heads_done, used)
                act.activation(o_sb[:, g % 2, :], o_ps[:], ACT.Copy).then_inc(o_copied, 1)

            def load_den(i, g):
                copied, inverted = counts(act, NG * i + g + 1, NG * i + g)
                act.wait_ge(o_copied, copied)
                act.wait_ge(den_inverted, inverted)
                act.dma_start(den[:], o_sb[HD:P:32, g % 2, :]).then_inc(den_loaded, DMA)

            def squares(n, tiles):
                normal, read = counts(act, n + 1, n)
                act.wait_ge(ln2_done, normal)
                act.wait_ge(ms_done, read)
                for t in tiles:
                    act.activation(sq[:], xn2[:, t, :], ACT.Square, accum_out=ssq[:, t:t + 1]).then_inc(ssq_done, 1)
                    act.wait_ge(ssq_done, count(act, TT * n + t + 1))

            def x2t_part(n, c):
                ready, stored, used = counts(act, CT * n + c + 1, DMA * n, n)
                act.wait_ge(x2t_ready, ready)
                act.wait_ge(x2t_stored, stored)
                act.wait_ge(logits_ready, used)
                act.activation(x2t[:, c, :], m_ps[:], ACT.Copy).then_inc(x2t_copied, 1)

            def copy_logits(n):
                act.wait_ge(logits_ready, count(act, n + 1))
                act.activation(lgt[:], m_ps[:, 0:P], ACT.Copy).then_inc(lgt_copied, 1)

            def gap_exp(n):
                act.wait_ge(gap_known, count(act, n + 1))
                act.activation(gap[:, 1, :], gap[:, 0, :], ACT.Exp).then_inc(gap_exp_done, 1)

            def body(i, first, last):
                for s in range(NH):
                    g = s // GRP
                    exps(i, s, 0)
                    if s == 11 and not first:
                        x2t_part(i - 1, 1)
                    if s == 11 and not first:
                        squares(i - 1, (2,))
                    exps(i, s, 1)
                    if s == 11 and not first:
                        squares(i - 1, (3,))
                    if s % 2 == 0 and not (last and s == 14):
                        mt_hi_part(i, s // 2 + 1)
                    exps(i, s, 2)
                    group_done = s % GRP == GRP - 1 and not (first and g == 0)
                    if group_done:
                        copy_o(i, g - 1)
                    if not last:
                        if s in XT_SLOTS:
                            xt_hi_part(i + 1, XT_SLOTS.index(s))
                        if s in QK_SLOTS:
                            qk_read_part(i + 1, QK_SLOTS.index(s))
                        if s in V_SLOTS:
                            v_read(i + 1, V_SLOTS.index(s))
                    if not first:
                        if s == 10:
                            x2t_part(i - 1, 0)
                        if s == 11:
                            copy_logits(i - 1)
                        if s == 14:
                            gap_exp(i - 1)
                    exps(i, s, 3)
                    if group_done:
                        load_den(i, g - 1)
                    if s in QK_SLOTS and not last:
                        qk_hi_part(i + 1, QK_SLOTS.index(s))
                    if s == 10 and not first:
                        squares(i - 1, (0, 1))

            xt_hi_part(0, 0)
            xt_hi_part(0, 1)
            act.wait_ge(bias_loaded, DMA * 9)
            for m in range(4):
                qk_read_part(0, m)
                qk_hi_part(0, m)
            v_read(0, 0)
            v_read(0, 1)
            mt_hi_part(0, 0)
            body(0, True, False)
            with act.Fori(1, NB - 1) as i:
                body(i, False, False)
            body(NB - 1, False, True)
            copy_o(NB - 1, NG - 1)
            load_den(NB - 1, NG - 1)
            act.wait_ge(s_exp_ready, KT * NH * NB)
            act.wait_ge(keep["raw_loaded"], 3 * DMA)
            for n in range(PIECES):
                for k, cols in piece_parts(n):
                    act.activation(keep["w_hi"][0][k][:, cols], flat(keep["raw"][0][k])[:, cols],
                                   ACT.Copy).then_inc(keep["w_hi_done"], 1)
            squares(NB - 1, range(TT))
            x2t_part(NB - 1, 0)
            x2t_part(NB - 1, 1)
            copy_logits(NB - 1)
            gap_exp(NB - 1)

        @block.vector
        def _(dve):
            dve.memset(wp[:], 0.0).then_inc(wp_zeroed, 1)
            dve.memset(rwt[:], 0.0).then_inc(dve_consts, 1)
            for h in range(2):
                dve.memset(q_st[h][0:96, :, :].bitcast(F32), 0.0).then_inc(dve_consts, 1)
                dve.memset(k_st[h][0:96, :, :].bitcast(F32), -1.0).then_inc(dve_consts, 1)
            dve.memset(v_aug[:], 1.0).then_inc(dve_consts, 1)
            dve.memset(base[:], 0.0).then_inc(dve_consts, 1)

            def ln_stats(half, src, st, steps):
                for t in (2 * half, 2 * half + 1):
                    dve.bn_stats(st[:, t, :], src[:, t, :]).then_inc(steps, 1)

            def ln_means(n, st, mv, steps, stats):
                made, known = counts(dve, 7, 2 * TT * n + TT)
                dve.wait_ge(dve_consts, made)
                dve.wait_ge(steps, known)
                for t in range(TT):
                    dve.bn_aggr(mv[:, t, :], st[:, t, :]).then_inc(steps, 1)
                dve.wait_ge(steps, count(dve, 2 * TT * n + 2 * TT))
                dve.tensor_scalar(mv[:, :, 1], mv[:, :, 1], LN_EPS, None, ALU.add).then_inc(stats, 1)

            def ln1_stats_of(n, half):
                if half == 0:
                    dve.wait_ge(x_loaded, count(dve, DMA * (n + 1)))
                ln_stats(half, xs, st1, ln1_steps)

            def ln1_means(n):
                ln_means(n, st1, mv1, ln1_steps, ln1_stats)

            def ln1_b(n):
                dve.wait_ge(ln1_rstd, count(dve, n + 1))
                for t in range(TT):
                    ins = dve.tensor_scalar(xn[:, t, :], xs[:, t, :], mv1[:, t, 0:1], rstd1[:, t:t + 1],
                                            ALU.subtract, ALU.mult)
                ins.then_inc(ln1_done, 1)

            def xt_lo_part(n, c):
                dve.wait_ge(xt_hi_done, count(dve, CT * n + c + 1))
                dve.tensor_tensor(xt_lo[:, c, :], m_ps[:], xt_hi[:, c, :].bitcast(F32),
                                  ALU.subtract).then_inc(xt_split, 1)

            def row_max(i, s, q):
                dve.wait_ge(s_max_ready, count(dve, TT * (NH * i + s) + q + 1))
                dve.tensor_reduce(mx[:, (s // 2) % 2, TT * (s % 2) + q:TT * (s % 2) + q + 1], s_max[q][:],
                                  AX.X, ALU.max).then_inc(max_done, 1)

            def mt_lo_part(i, c):
                dve.wait_ge(mt_hi_done, count(dve, PAIRS * i + c + 1))
                dve.tensor_tensor(mt_lo[:, c % 2, :], m_ps[0:2 * TT, 0:P], mt_hi[:, c % 2, :].bitcast(F32),
                                  ALU.subtract).then_inc(mt_split, 1)

            def invert_den(i, g):
                loaded, stored = counts(dve, DMA * (NG * i + g + 1), DMA * (NG * i + g))
                dve.wait_ge(den_loaded, loaded)
                dve.wait_ge(recip_stored, stored)
                dve.reciprocal(rden[:], den[:]).then_inc(den_inverted, 1)

            def add_x(n, t):
                ready, loaded = counts(dve, 2 * n + t + 1, DMA * (n + 1))
                dve.wait_ge(proj_ready, ready)
                dve.wait_ge(xr_loaded, loaded)
                part = xr[:, 2 * t:2 * t + 2, :]
                dve.tensor_tensor(part, m_ps[:].rearrange("p (t c) -> p t c", t=2), part, ALU.add).then_inc(x1_done, 1)

            def ln2_stats_of(n, half):
                dve.wait_ge(x1_done, count(dve, 2 * n + half + 1))
                ln_stats(half, xr, st2, ln2_steps)

            def ln2_means(n):
                ln_means(n, st2, mv2, ln2_steps, ln2_stats)

            def ln2_b(n):
                ready, sent = counts(dve, n + 1, DMA * 2 * TT * n)
                dve.wait_ge(ln2_rstd, ready)
                dve.wait_ge(rows_sent, sent)
                for t in range(TT):
                    ins = dve.tensor_scalar(xn2[:, t, :], xr[:, t, :], mv2[:, t, 0:1], rstd2[:, t:t + 1],
                                            ALU.subtract, ALU.mult)
                ins.then_inc(ln2_done, 1)

            def over_experts(ap):
                return ap.rearrange("p (t a) -> p t a", a=1).to_broadcast([P, TT, NE])

            def for_both(tensor):
                return tensor[:].rearrange("p (a t) e -> p a (t e)", a=1).to_broadcast([P, 2, TT * NE])

            def by_expert(ap):
                return ap.rearrange("p (t e) -> p t e", e=NE)

            def read_logits(n):
                ready, known = counts(dve, n + 1, n + 1)
                dve.wait_ge(lg_ready, ready)
                dve.wait_ge(rms_done, known)
                dve.tensor_tensor(lg[:], m_ps[:, 0:P].rearrange("p (t e) -> p t e", t=TT)[:, :, 0:NE],
                                  over_experts(rrms[:]), ALU.mult).then_inc(logits_read, 1)

            def choose(n, k):
                done = CHOICE_STEPS * n + 6 * k
                if k == 0:
                    dve.wait_ge(logits_read, count(dve, n + 1))
                else:
                    dve.wait_ge(choice_steps, count(dve, done))
                dve.tensor_reduce(top[:, k, :], lg[:], AX.X, ALU.max).then_inc(choice_steps, 1)
                dve.wait_ge(choice_steps, count(dve, done + 1))
                dve.tensor_tensor(key[:], lg[:], over_experts(top[:, k, :]), ALU.is_equal).then_inc(choice_steps, 1)
                dve.wait_ge(choice_steps, count(dve, done + 2))
                dve.tensor_tensor(key[:], key[:], rank[:], ALU.mult).then_inc(choice_steps, 1)
                dve.wait_ge(choice_steps, count(dve, done + 3))
                dve.tensor_reduce(best[:], key[:], AX.X, ALU.max).then_inc(choice_steps, 1)
                dve.wait_ge(choice_steps, count(dve, done + 4))
                dve.tensor_tensor(by_expert(chosen[:, k, :]), key[:], over_experts(best[:]),
                                  ALU.is_equal).then_inc(choice_steps, 1)
                dve.wait_ge(choice_steps, count(dve, done + 5))
                if k == 0:
                    dve.scalar_tensor_tensor(out=lg[:], in0=by_expert(chosen[:, 0, :]), scalar=-3.0e38, in1=lg[:],
                                             op0=ALU.mult, op1=ALU.add).then_inc(choice_steps, 1)
                else:
                    dve.tensor_tensor(mask[:], chosen[:, 0, :], chosen[:, 1, :], ALU.add).then_inc(mask_done, 1)
                    dve.tensor_tensor(gap[:, 0, :], top[:, 1, :], top[:, 0, :], ALU.subtract).then_inc(gap_known, 1)

            CHOICE_STEPS = 11

            def read_positions(n):
                done = SLOT_STEPS * n
                dve.wait_ge(pos_ready, count(dve, n + 1))
                for t in range(TT):
                    dve.tensor_tensor(pos[:, t, :], m_ps[:, NE * t:NE * t + NE], base[:], ALU.add).then_inc(slot_steps, 1)
                    dve.tensor_tensor(base[:], base[:], m_ps[:, NE * (TT + t):NE * (TT + t) + NE],
                                      ALU.add).then_inc(slot_steps, 1)
                    done = done + 2
                    dve.wait_ge(slot_steps, count(dve, done))
                dve.scalar_tensor_tensor(out=slot_all[:], in0=expert_no[:], scalar=float(CAP), in1=pos[:],
                                         op0=ALU.mult, op1=ALU.add).then_inc(pos_read, 1)

            def number(n):
                done = SLOT_STEPS * n + 2 * TT
                dve.wait_ge(pos_read, count(dve, n + 1))
                dve.tensor_tensor(picks[:], chosen[:], for_both(pos), ALU.mult).then_inc(slot_steps, 1)
                dve.wait_ge(slot_steps, count(dve, done + 1))
                dve.tensor_reduce(place[:], picks[:].rearrange("p k (t e) -> p k t e", e=NE), AX.X,
                                  ALU.add).then_inc(slot_steps, 1)
                dve.wait_ge(slot_steps, count(dve, done + 2))
                dve.tensor_tensor(picks[:], chosen[:], for_both(slot_all), ALU.mult).then_inc(slot_steps, 1)
                dve.wait_ge(slot_steps, count(dve, done + 3))
                dve.tensor_reduce(slot[:], picks[:].rearrange("p k (t e) -> p k t e", e=NE), AX.X,
                                  ALU.add).then_inc(slot_steps, 1)
                dve.tensor_scalar(place[:], place[:], float(CAP), None, ALU.is_lt).then_inc(slot_steps, 1)
                dve.wait_ge(slot_steps, count(dve, done + 5))
                dve.scalar_tensor_tensor(out=slot[:], in0=slot[:], scalar=-float(SLOTS), in1=place[:],
                                         op0=ALU.add, op1=ALU.mult).then_inc(slot_steps, 1)
                dve.wait_ge(slot_steps, count(dve, done + 6))
                dve.tensor_scalar(slot[:], slot[:], float(SLOTS), None, ALU.add).then_inc(slot_steps, 1)
                sent, last = counts(dve, DMA * 2 * TT * n, done + 7)
                dve.wait_ge(rows_sent, sent)
                dve.wait_ge(slot_steps, last)
                dve.tensor_copy(row_no[:], slot[:]).then_inc(rows_known, 1)
                dve.tensor_copy(keep["row_no"][:, bass.ds(n, 1), :, :].rearrange("p n k t -> p (n k) t"),
                                slot[:]).then_inc(slot_steps, 1)

            def weigh(n):
                done = SLOT_STEPS * n + 2 * TT
                dve.wait_ge(gap_exp_done, count(dve, n + 1))
                dve.tensor_scalar(total[:], gap[:, 1, :], 1.0, None, ALU.add).then_inc(slot_steps, 1)
                dve.wait_ge(slot_steps, count(dve, done + 9))
                dve.reciprocal(share[:, 0, :], total[:]).then_inc(slot_steps, 1)
                dve.wait_ge(slot_steps, count(dve, done + 10))
                dve.tensor_tensor(share[:, 1, :], gap[:, 1, :], share[:, 0, :], ALU.mult).then_inc(slot_steps, 1)
                dve.wait_ge(slot_steps, count(dve, done + 11))
                dve.tensor_tensor(keep["choice_w"][:, bass.ds(n, 1), :, :].rearrange("p n k t -> p (n k) t"),
                                  share[:], place[:], ALU.mult).then_inc(slot_steps, 1)

            SLOT_STEPS = 2 * TT + 12

            def body(i, first, last, more_x):
                for s in range(NH):
                    g, j = s // GRP, s % GRP
                    later_max = not (last and s + GRP >= NH)
                    if later_max:
                        row_max(i, s + GRP, 0)
                        row_max(i, s + GRP, 1)
                    if s == 12 and not first:
                        read_logits(i - 1)
                    if s % 2 == 0 and not (last and s == 14):
                        mt_lo_part(i, s // 2 + 1)
                    if not first:
                        if s == 13:
                            choose(i - 1, 1)
                        if s == 15:
                            number(i - 1)
                    if later_max:
                        row_max(i, s + GRP, 2)
                        row_max(i, s + GRP, 3)
                    if j == 0 and (not first or g >= 2):
                        invert_den(i, g - 2)
                    if not first:
                        if s in PROJ_SLOTS:
                            add_x(i - 1, PROJ_SLOTS.index(s))
                            ln2_stats_of(i - 1, PROJ_SLOTS.index(s))
                        if s == PROJ_SLOTS[1]:
                            ln2_means(i - 1)
                        if s == 9:
                            ln2_b(i - 1)
                        if s == 12:
                            choose(i - 1, 0)
                        if s == 14:
                            read_positions(i - 1)
                    if not last:
                        if s in XT_SLOTS:
                            xt_lo_part(i + 1, XT_SLOTS.index(s))
                    if s == 15 and not first:
                        weigh(i - 1)
                    if more_x:
                        if s in (2, 4):
                            ln1_stats_of(i + 2, s // 4)
                        if s == 5:
                            ln1_means(i + 2)
                        if s == 6:
                            ln1_b(i + 2)

            for half in range(2):
                ln1_stats_of(0, half)
            ln1_means(0)
            ln1_b(0)
            for c in range(CT):
                for part in range(2):
                    dve.wait_ge(wq_hi_done, 3 * c + part + 1)
                    src = wq_raw[:, c, part * C:(part + 1) * C].rearrange("p (r j d) -> p r d j", j=2, d=HD)
                    hi = wq_hi[:, c, part * C:(part + 1) * C].rearrange("p (r d j) -> p r d j", j=2, d=HD)
                    lo = wq_lo[:, c, part * C:(part + 1) * C].rearrange("p (r d j) -> p r d j", j=2, d=HD)
                    dve.tensor_tensor(lo, src, hi.bitcast(F32), ALU.subtract).then_inc(wq_lo_done, 1)
                dve.wait_ge(wq_hi_done, 3 * c + 3)
                dve.tensor_tensor(wq_lo[:, c, 2 * C:], wq_raw[:, c, 2 * C:], wq_hi[:, c, 2 * C:].bitcast(F32),
                                  ALU.subtract).then_inc(wq_lo_done, 1)
            dve.wait_ge(rwt_ready, 1)
            dve.tensor_copy(rwt[:, :, 0:NE], m_ps[:, 0:CT * NE].rearrange("p (c e) -> p c e", c=CT)).then_inc(rwt_copied, 1)
            xt_lo_part(0, 0)
            xt_lo_part(0, 1)
            for s in range(GRP):
                for q in range(TT):
                    row_max(0, s, q)
                if s == 1:
                    mt_lo_part(0, 0)
            for half in range(2):
                ln1_stats_of(1, half)
            ln1_means(1)
            ln1_b(1)
            body(0, True, False, True)
            with dve.Fori(1, NB - 2) as i:
                body(i, False, False, True)
            body(NB - 2, False, False, False)
            body(NB - 1, False, True, False)
            invert_den(NB - 1, 2)
            invert_den(NB - 1, 3)
            for n in range(PIECES):
                for m, (k, cols) in enumerate(piece_parts(n)):
                    dve.wait_ge(keep["w_hi_done"], PARTS_BEFORE[n] + m + 1)
                    dve.tensor_tensor(keep["w_lo"][0][k][:, cols], flat(keep["raw"][0][k])[:, cols],
                                      keep["w_hi"][0][k][:, cols].bitcast(F32), ALU.subtract).then_inc(keep["w_split"], 1)
            for half in range(2):
                add_x(NB - 1, half)
                ln2_stats_of(NB - 1, half)
            ln2_means(NB - 1)
            ln2_b(NB - 1)
            read_logits(NB - 1)
            choose(NB - 1, 0)
            choose(NB - 1, 1)
            read_positions(NB - 1)
            number(NB - 1)
            weigh(NB - 1)

        @block.tensor
        def _(pe):
            bank = Reader()

            def front_xt(n, c):
                ready, emptied = counts(pe, n + 1, bank.value)
                pe.wait_ge(ln1_done, ready)
                pe.wait_ge(bank.sem, emptied)
                for t in range(TT):
                    ins = pe.transpose(m_ps[:, P * t:P * t + P], xn[:, t, P * c:P * c + P], ident[:])
                ins.then_inc(xt_ready, 1)
                bank.is_(xt_split, CT * n + c + 1)

            def front_qk(n, m):
                split, emptied = counts(pe, CT * n + CT, bank.value)
                pe.wait_ge(xt_split, split)
                pe.wait_ge(bank.sem, emptied)
                cols = slice((m % 2) * C + (m // 2) * P, (m % 2) * C + (m // 2) * P + P)
                parts = [(w[:, c, cols], xp[:, c, :]) for c in range(CT)
                         for w, xp in ((wq_hi, xt_hi), (wq_hi, xt_lo), (wq_lo, xt_hi))]
                for k, (w, xp) in enumerate(parts):
                    ins = pe.matmul(m_ps[:], w, xp, start=(k == 0), stop=(k == len(parts) - 1))
                ins.then_inc(qk_ready, 1)
                bank.is_(qk_read, 4 * n + m + 1)

            def front_v(n, h):
                pe.wait_ge(bank.sem, count(pe, bank.value))
                for t in (2 * h, 2 * h + 1):
                    out = m_ps[:, C * (t % 2):C * (t % 2) + C]
                    parts = [(xp[:, c, P * t:P * t + P], w[:, c, 2 * C:]) for c in range(CT)
                             for xp, w in ((xt_hi, wq_hi), (xt_hi, wq_lo), (xt_lo, wq_hi))]
                    for k, (xp, w) in enumerate(parts):
                        ins = pe.matmul(out, xp, w, start=(k == 0), stop=(k == len(parts) - 1))
                ins.then_inc(v_ready, 1)
                bank.is_(v_there, 2 * n + h + 1)

            def scores_max(i, s, q):
                reduced, loaded = counts(pe, TT * (NH * i + s) + q - 3,
                                         6 * DMA * ((PAIRS // 2) * i + s // 4 + 1))
                if q == 0 and s % 2 == 0:
                    pe.wait_ge(pair_loaded[(s // 2) % 2], loaded)
                pe.wait_ge(max_done, reduced)
                half, ring = (s // 4) % 2, s % 4
                pe.matmul(s_max[q][:], q_st[half][0:ROWS_MAX, ring, P * q:P * q + P],
                          k_st[half][0:ROWS_MAX, ring, :], start=True, stop=True).then_inc(s_max_ready, 1)

            def scores_exp(i, s, k):
                read, loaded = counts(pe, KT * (NH * i + s) + k - 1, 2 * DMA * ((PAIRS // 2) * i + s // 4 + 1))
                if k == 0 and s % 2 == 0:
                    pe.wait_ge(max_loaded[(s // 2) % 2], loaded)
                pe.wait_ge(exp_done, read)
                half, ring = (s // 4) % 2, s % 4
                pe.matmul(s_exp[k % 2][:], k_st[half][0:ROWS_EXP, ring, P * k:P * k + P],
                          q_st[half][0:ROWS_EXP, ring, :], start=True, stop=True).then_inc(s_exp_ready, 1)

            def pv(i, g, k):
                heads_before = NH * i + GRP * g + GRP - 1
                probs_made, v_there, emptied = counts(pe, KT * heads_before + k + 1, NG * i + g + 1, NG * i + g)
                pe.wait_ge(exp_done, probs_made)
                if k == 0:
                    pe.wait_ge(v_copied, v_there)
                    pe.wait_ge(o_copied, emptied)
                for j in range(GRP):
                    ins = pe.matmul(o_ps[32 * j:32 * j + 32, :], v_aug[:, k, (GRP * g + j) % NH, :],
                                    probs[:, g % 2, j, k, :], start=(k == 0), stop=(k == KT - 1))
                if k == KT - 1:
                    ins.then_inc(pv_done, 1)

            def max_t(i, c):
                reduced, emptied = counts(pe, 2 * TT * (PAIRS * i + c + 1), bank.value)
                pe.wait_ge(max_done, reduced)
                pe.wait_ge(bank.sem, emptied)
                pe.transpose(m_ps[0:2 * TT, 0:P], mx[:, c % 2, :], ident[:]).then_inc(mt_ready, 1)
                bank.is_(mt_split, PAIRS * i + c + 1)

            def project(n, h):
                normal, emptied = counts(pe, NG * n + NG, bank.value)
                pe.wait_ge(heads_done, normal)
                pe.wait_ge(bank.sem, emptied)
                for t in (2 * h, 2 * h + 1):
                    for g in range(NG):
                        ins = pe.matmul(m_ps[:, C * (t % 2):C * (t % 2) + C], heads[:, g, P * t:P * t + P],
                                        wp[:, g, :], start=(g == 0), stop=(g == NG - 1))
                ins.then_inc(proj_ready, 1)
                bank.is_(x1_done, 2 * n + h + 1)

            def back_xt(n, c):
                normal, emptied = counts(pe, n + 1, bank.value)
                pe.wait_ge(ln2_done, normal)
                pe.wait_ge(bank.sem, emptied)
                for t in range(TT):
                    ins = pe.transpose(m_ps[:, P * t:P * t + P], xn2[:, t, P * c:P * c + P], ident[:])
                ins.then_inc(x2t_ready, 1)
                bank.is_(x2t_copied, CT * n + c + 1)

            def logits(n):
                copied, emptied = counts(pe, CT * n + CT, bank.value)
                pe.wait_ge(x2t_copied, copied)
                pe.wait_ge(bank.sem, emptied)
                for c in range(CT):
                    for t in range(TT):
                        ins = pe.matmul(m_ps[32 * t:32 * t + 32, 0:P], rwt[:, c, :], x2t[:, c, P * t:P * t + P],
                                        start=(c == 0), stop=(c == CT - 1))
                ins.then_inc(logits_ready, 1)

            def logits_t(n):
                pe.wait_ge(lgt_copied, count(pe, n + 1))
                pe.transpose(m_ps[:, 0:P], lgt[:], ident[:]).then_inc(lg_ready, 1)
                bank.is_(logits_read, n + 1)

            def positions(n):
                known, emptied = counts(pe, n + 1, bank.value)
                pe.wait_ge(mask_done, known)
                pe.wait_ge(bank.sem, emptied)
                pe.matmul(m_ps[:, 0:TT * NE], before[:], mask[:], start=True, stop=True)
                pe.matmul(m_ps[:, TT * NE:2 * TT * NE], ones[:], mask[:], start=True, stop=True).then_inc(pos_ready, 1)
                bank.is_(pos_read, n + 1)

            def body(i, first, last):
                for s in range(NH):
                    later_max = not (last and s + GRP >= NH)
                    if later_max:
                        scores_max(i, s + GRP, 0)
                        scores_max(i, s + GRP, 1)
                    scores_exp(i, s, 0)
                    if not first:
                        if s == 11:
                            back_xt(i - 1, 1)
                        if s == 12:
                            logits_t(i - 1)
                    if later_max:
                        scores_max(i, s + GRP, 2)
                    scores_exp(i, s, 1)
                    if s % 2 == 0 and not (last and s == 14):
                        max_t(i, s // 2 + 1)
                    if later_max:
                        scores_max(i, s + GRP, 3)
                    if not (first and s < GRP):
                        pv(i, s // GRP - 1, s % GRP)
                    scores_exp(i, s, 2)
                    if not last:
                        if s in XT_SLOTS:
                            front_xt(i + 1, XT_SLOTS.index(s))
                        if s in QK_SLOTS:
                            front_qk(i + 1, QK_SLOTS.index(s))
                        if s in V_SLOTS:
                            front_v(i + 1, V_SLOTS.index(s))
                    if not first:
                        if s in PROJ_SLOTS:
                            project(i - 1, PROJ_SLOTS.index(s))
                        if s == 10:
                            back_xt(i - 1, 0)
                        if s == 11:
                            logits(i - 1)
                        if s == 14:
                            positions(i - 1)
                    scores_exp(i, s, 3)

            pe.wait_ge(consts_made, 9)
            pe.wait_ge(rw_loaded, DMA)
            for c in range(CT):
                ins = pe.transpose(m_ps[:, NE * c:NE * c + NE], rw_raw[:, P * c:P * c + P], ident[0:NE, 0:NE])
            ins.then_inc(rwt_ready, 1)
            bank.is_(rwt_copied, 1)
            front_xt(0, 0)
            front_xt(0, 1)
            pe.wait_ge(wq_lo_done, 3 * CT)
            for m in range(4):
                front_qk(0, m)
            front_v(0, 0)
            front_v(0, 1)
            pe.wait_ge(dve_consts, 7)
            for s in range(GRP):
                for q in range(TT):
                    scores_max(0, s, q)
                if s == 1:
                    max_t(0, 0)
            pe.wait_ge(wp_loaded, 5 * DMA)
            body(0, True, False)
            with pe.Fori(1, NB - 1) as i:
                bank.is_(qk_read, 4 * i + 4)
                body(i, False, False)
            bank.is_(qk_read, 4 * (NB - 1) + 4)
            body(NB - 1, False, True)
            for k in range(KT):
                pv(NB - 1, NG - 1, k)
            project(NB - 1, 0)
            project(NB - 1, 1)
            back_xt(NB - 1, 0)
            back_xt(NB - 1, 1)
            logits(NB - 1)
            logits_t(NB - 1)
            positions(NB - 1)


TILE = SEQ
SPLIT = (384, 256)
E0, Z0 = NB, NB + 2 * NE
END = Z0 + NB


class Tile:

    def __init__(self, kind, index, half=0, odd=0):
        self.kind, self.index, self.half = kind, index, half
        if kind == "first":
            self.no, self.job, self.set, self.cols = index, 0, 0, TILE
        elif kind == "expert":
            self.no, self.job, self.set, self.cols = E0 + 2 * index + half, 1 + index, 1 - odd, SPLIT[half]
        else:
            self.no, self.job, self.set, self.cols = Z0 + index, 1 + NE, (1 + NE) % 2, TILE
        self.rows = self.cols // P


def all_tiles(eng, tile):
    def firsts(n, first, last):
        a, b = Tile("first", 2 * n), Tile("first", 2 * n + 1)
        tile(None if first else Tile("first", 2 * n - 1), a, b, 0, (), None)
        tile(a, b, Tile("expert", 0) if last else Tile("first", 2 * n + 2), 1, range(PIECES) if last else (), 1)

    def experts(n, first, last):
        before = Tile("first", NB - 1) if first else Tile("expert", 2 * n - 1, 1, 1)
        for odd in range(2):
            e = 2 * n + odd
            a, b = Tile("expert", e, 0, odd), Tile("expert", e, 1, odd)
            after = Tile("last", 0) if last and odd else Tile("expert", e + 1, 0, 1 - odd)
            tile(before, a, b, 0, range(0, PIECES // 2), e + 2)
            tile(a, b, after, 1, range(PIECES // 2, PIECES), e + 2)
            before = b

    def lasts(n, first, last):
        a, b = Tile("last", 2 * n), Tile("last", 2 * n + 1)
        tile(Tile("expert", NE - 1, 1, 1) if first else Tile("last", 2 * n - 1), a, b, 0, (), None)
        tile(a, b, None if last else Tile("last", 2 * n + 2), 1, (), None)

    for part, turns in ((firsts, NB // 2), (experts, NE // 2), (lasts, NB // 2)):
        part(0, True, False)
        with eng.Fori(1, turns - 1) as n:
            part(n, False, False)
        part(turns - 1, False, True)


def ffn_block(nc, sg, su, sd, rg, ru, rd, x1_dram, x2t_dram, slots_dram, rows_dram, keep, out):
    assert sum(SPLIT) == CAP and NB % 2 == 0 and NE % 2 == 0
    with ExitStack() as ctx:
        def sb(name, shape, dt=F32):
            return ctx.enter_context(nc.sbuf_tensor(name, shape, dt))

        def psum(name, cols):
            return ctx.enter_context(nc.psum_tensor(name, [P, cols], F32))

        def sem(name):
            return ctx.enter_context(nc.semaphore(name))

        ident = keep["ident"]
        raw = [keep["raw"][0], [sb("raw1_g", [P, CT, IR]), sb("raw1_u", [P, CT, IR]), sb("raw1_d", [P, FT, C])]]
        w_hi = [keep["w_hi"][0], [sb(f"w_hi1_{k}", [P, CT * IR], F32R) for k in range(3)]]
        w_lo = [keep["w_lo"][0], [sb(f"w_lo1_{k}", [P, CT * IR], F32R) for k in range(3)]]
        xt = sb("xt", [P, CT, TILE])
        xrow = flat(xt)[:, 0:SPLIT[0] // P * C].rearrange("p (t c) -> p t c", c=C)
        t_hi = [sb(f"t_hi{n}", [P, CT, TILE], F32R) for n in range(2)]
        t_lo = [sb(f"t_lo{n}", [P, CT, TILE], F32R) for n in range(2)]
        hid = [sb(f"hid{n}", [P, TILE]) for n in range(4)]
        h_hi = [sb(f"h_hi{n}", [P, TILE], F32R) for n in range(4)]
        h_lo = [sb(f"h_lo{n}", [P, TILE], F32R) for n in range(4)]
        ys = [sb(f"ys{n}", [P, TT, C]) for n in range(2)]
        x1 = sb("x1", [P, TT, C])
        picked = flat(raw[1][0]).rearrange("p (k t c) -> p k t c", k=2, t=TT)
        pick_no = sb("pick_no", [P, 2, TT], U32)
        pick_w = sb("pick_w", [P, 2, TT])

        gate = [psum(f"gate{n}", SEQ) for n in range(2)]
        up = [psum(f"up{n}", SEQ) for n in range(2)]
        y_ps = [psum(f"y_ps{n}", 2 * SEQ) for n in range(2)]

        raw_loaded, w_hi_done, w_split = keep["raw_loaded"], keep["w_hi_done"], keep["w_split"]
        tile_loaded = sem("tile_loaded")
        tile_t = sem("tile_t")
        tile_hi = sem("tile_hi")
        tile_split = sem("tile_split")
        gate_up_ready = sem("gate_up_ready")
        silu_done = sem("silu_done")
        hid_done = sem("hid_done")
        hid_hi = sem("hid_hi")
        hid_split = sem("hid_split")
        hid_used = sem("hid_used")
        y_read = sem("y_read")
        y_done = sem("y_done")
        y_stored = sem("y_stored")
        x1_loaded = sem("x1_loaded")
        picks_copied = sem("picks_copied")
        picked_rows = sem("picked_rows")
        sum_steps = sem("sum_steps")
        SUM_STEPS = 2 * TT - 1

        x1v = x1_dram.rearrange("(b t p) c -> b p t c", p=P, t=TT)
        outv = out.rearrange("b (t p) c -> b p t c", p=P)
        x2tv = x2t_dram.rearrange("(c p) t -> p c t", p=P)

        block = ctx.enter_context(nc.Block())

        @block.sync
        def _(sp):
            sgv, suv = (w.rearrange("(c p) n -> p c n", p=P) for w in (sg, su))
            sdv = sd.rearrange("(f p) n -> p f n", p=P)
            expert_w = (rg.rearrange("e (c p) n -> e p c n", p=P), ru.rearrange("e (c p) n -> e p c n", p=P),
                        rd.rearrange("e (f p) n -> e p f n", p=P))

            def load_weights(job, parity):
                sp.wait_ge(w_split, count(sp, PARTS * (job - 1)))
                if isinstance(job, int) and job == 1 + NE:
                    srcs = (sgv[:, :, IR:], suv[:, :, IR:], sdv[:, FT:, :])
                else:
                    srcs = tuple(one_batch(v, job - 1) for v in expert_w)
                for dst, src in zip(raw[parity], srcs):
                    sp.dma_start(dst[:], src).then_inc(raw_loaded, DMA)

            def slot_rows(t, table):
                first = CAP * t.index + SPLIT[0] * t.half
                return table[bass.ds(first, t.cols), :].rearrange("(t p) c -> p t c", p=P)

            def load_tile(t):
                sp.wait_ge(tile_split, count(sp, CT * t.no))
                if t.kind == "expert":
                    if isinstance(t.index, int) and t.index + t.half == 0:
                        sp.wait_ge(keep["rows_sent"], DMA * 2 * TT * NB)
                    sp.dma_start(xrow[:, 0:t.rows, :], slot_rows(t, slots_dram)).then_inc(tile_loaded, DMA)
                else:
                    sp.dma_start(xt[:], x2tv[:, :, bass.ds(t.index * TILE, TILE)]).then_inc(tile_loaded, DMA)

            def store_tile(t, parity):
                sp.wait_ge(y_done, count(sp, t.no + 1))
                if t.kind == "first":
                    sp.dma_start(one_batch(x1v, t.index), ys[parity][:]).then_inc(y_stored, DMA)
                elif t.kind == "expert":
                    sp.dma_start(slot_rows(t, rows_dram), ys[parity][:, 0:t.rows, :]).then_inc(y_stored, DMA)
                else:
                    sp.dma_start(one_batch(outv, t.index), ys[parity][:]).then_inc(y_stored, DMA)

            def tile(before, t, after, parity, pieces, job):
                if t.kind == "expert" and t.half == 0 and not (isinstance(t.index, int) and t.index + 3 > 1 + NE):
                    load_weights(t.index + 3, t.set)
                if after:
                    load_tile(after)
                if before:
                    store_tile(before, 1 - parity)
                if t.kind != "expert":
                    if not before or before.kind == "expert":
                        sp.wait_ge(y_stored, count(sp, DMA * t.no))
                    sp.wait_ge(y_done, count(sp, t.no))
                    sp.dma_start(x1[:], one_batch(x1v, t.index)).then_inc(x1_loaded, DMA)

            load_tile(Tile("first", 0))
            load_weights(1, 1)
            load_weights(2, 0)
            all_tiles(sp, tile)
            store_tile(Tile("last", NB - 1), 1)
            sp.wait_ge(y_stored, DMA * END)

        @block.gpsimd
        def _(pool):
            send_rows(pool, slots_dram, keep)
            with pool.Fori(0, NB) as n:
                stored, used = counts(pool, DMA * Z0, Z0 + n)
                pool.wait_ge(y_stored, stored)
                pool.wait_ge(y_done, used)
                pool.tensor_copy(pick_no[:], keep["row_no"][:, bass.ds(n, 1), :, :].rearrange("p n k t -> p (n k) t")
                                 ).then_inc(picks_copied, 1)
                pool.tensor_copy(pick_w[:], keep["choice_w"][:, bass.ds(n, 1), :, :].rearrange("p n k t -> p (n k) t")
                                 ).then_inc(picks_copied, 1)
                stored, copied = counts(pool, DMA * Z0, 2 * n + 2)
                pool.wait_ge(y_stored, stored)
                pool.wait_ge(picks_copied, copied)
                for t in range(TT):
                    for k in range(2):
                        pool.indirect_dma_start(
                            picked[:, k, t, :], None, rows_dram,
                            bass.IndirectOffsetOnAxis(ap=pick_no[:, k, t:t + 1], axis=0),
                            bounds_check=SLOTS, oob_is_err=False).then_inc(picked_rows, DMA)
            pool.wait_ge(picked_rows, DMA * 2 * TT * NB)

        @block.scalar
        def _(act):
            def tile_hi_part(t, parity):
                for c in range(CT):
                    if t.kind == "expert":
                        act.wait_ge(tile_t, count(act, CT * (t.no - E0) + c + 1))
                        src = y_ps[parity][:, SEQ * c:SEQ * c + t.cols]
                    else:
                        act.wait_ge(tile_loaded, count(act, DMA * (t.no + 1)))
                        src = xt[:, c, :]
                    act.activation(t_hi[parity][:, c, 0:t.cols], src, ACT.Copy).then_inc(tile_hi, 1)

            def tile(before, t, after, parity, pieces, job):
                per_step = len(pieces) // FT
                for f in range(FT):
                    no = FT * t.no + f
                    ready, split = counts(act, no + 1, no - 3)
                    act.wait_ge(gate_up_ready, ready)
                    act.wait_ge(hid_split, split)
                    act.activation(hid[f % 4][:, 0:t.cols], gate[f % 2][:, 0:t.cols], ACT.Silu).then_inc(silu_done, 1)
                    for n in pieces[per_step * f:per_step * (f + 1)]:
                        if n == 0:
                            act.wait_ge(raw_loaded, count(act, 3 * DMA * (job + 1)))
                        for k, cols in piece_parts(n):
                            act.activation(w_hi[1 - t.set][k][:, cols], flat(raw[1 - t.set][k])[:, cols],
                                           ACT.Copy).then_inc(w_hi_done, 1)
                    made, used = counts(act, no + 1, no - 3)
                    act.wait_ge(hid_done, made)
                    act.wait_ge(hid_used, used)
                    act.activation(h_hi[f % 4][:, 0:t.cols], hid[f % 4][:, 0:t.cols], ACT.Copy).then_inc(hid_hi, 1)
                    if f == 5 and after:
                        tile_hi_part(after, 1 - parity)

            tile_hi_part(Tile("first", 0), 0)
            all_tiles(act, tile)

        @block.vector
        def _(dve):
            def tile_lo_part(t, parity):
                for c in range(CT):
                    dve.wait_ge(tile_hi, count(dve, CT * t.no + c + 1))
                    src = y_ps[parity][:, SEQ * c:SEQ * c + t.cols] if t.kind == "expert" else xt[:, c, :]
                    dve.tensor_tensor(t_lo[parity][:, c, 0:t.cols], src, t_hi[parity][:, c, 0:t.cols].bitcast(F32),
                                      ALU.subtract).then_inc(tile_split, 1)

            def finish(t, parity):
                y = y_ps[parity][:, 0:C * t.rows].rearrange("p (t c) -> p t c", c=C)
                summed, stored = counts(dve, FT * (t.no + 1), DMA * (t.no - 1))
                dve.wait_ge(hid_used, summed)
                dve.wait_ge(y_stored, stored)
                if t.kind == "expert":
                    dve.tensor_copy(ys[parity][:, 0:t.rows, :], y).then_inc(y_done, 1)
                elif t.kind == "first":
                    dve.wait_ge(x1_loaded, count(dve, DMA * (t.index + 1)))
                    dve.tensor_tensor(ys[parity][:], y, x1[:], ALU.add).then_inc(y_done, 1)
                else:
                    dve.wait_ge(x1_loaded, count(dve, DMA * (NB + t.index + 1)))
                    dve.tensor_tensor(ys[parity][:], y, x1[:], ALU.add).then_inc(y_read, 1)
                    added, there = counts(dve, t.index + 1, DMA * 2 * TT * (t.index + 1))
                    dve.wait_ge(y_read, added)
                    dve.wait_ge(picked_rows, there)
                    for k in range(2):
                        for r in range(TT):
                            ins = dve.scalar_tensor_tensor(out=ys[parity][:, r, :], in0=picked[:, k, r, :],
                                                           scalar=pick_w[:, k, r:r + 1], in1=ys[parity][:, r, :],
                                                           op0=ALU.mult, op1=ALU.add)
                            if k == 1 and r == TT - 1:
                                ins.then_inc(y_done, 1)
                            else:
                                ins.then_inc(sum_steps, 1)
                        if k == 0:
                            dve.wait_ge(sum_steps, count(dve, SUM_STEPS * t.index + TT))

            def tile(before, t, after, parity, pieces, job):
                per_step = len(pieces) // FT
                for f in range(FT):
                    no = FT * t.no + f
                    dve.wait_ge(silu_done, count(dve, no + 1))
                    dve.tensor_tensor(hid[f % 4][:, 0:t.cols], up[f % 2][:, 0:t.cols], hid[f % 4][:, 0:t.cols],
                                      ALU.mult).then_inc(hid_done, 1)
                    for n in pieces[per_step * f:per_step * (f + 1)]:
                        for m, (k, cols) in enumerate(piece_parts(n)):
                            dve.wait_ge(w_hi_done, count(dve, PARTS * job + PARTS_BEFORE[n] + m + 1))
                            dve.tensor_tensor(w_lo[1 - t.set][k][:, cols], flat(raw[1 - t.set][k])[:, cols],
                                              w_hi[1 - t.set][k][:, cols].bitcast(F32), ALU.subtract).then_inc(w_split, 1)
                    dve.wait_ge(hid_hi, count(dve, no + 1))
                    dve.tensor_tensor(h_lo[f % 4][:, 0:t.cols], hid[f % 4][:, 0:t.cols],
                                      h_hi[f % 4][:, 0:t.cols].bitcast(F32), ALU.subtract).then_inc(hid_split, 1)
                    if f == 2 and before:
                        finish(before, 1 - parity)
                    if f == 5 and after:
                        tile_lo_part(after, 1 - parity)

            tile_lo_part(Tile("first", 0), 0)
            all_tiles(dve, tile)
            finish(Tile("last", NB - 1), 1)

        @block.tensor
        def _(pe):
            def transposes(t, parity):
                loaded, left = counts(pe, DMA * (t.no + 1), t.no - 1)
                pe.wait_ge(tile_loaded, loaded)
                pe.wait_ge(y_done, left)
                for c in range(CT):
                    for r in range(t.rows):
                        ins = pe.transpose(y_ps[parity][:, SEQ * c + P * r:SEQ * c + P * r + P],
                                           xrow[:, r, P * c:P * c + P], ident[:])
                    ins.then_inc(tile_t, 1)

            def gate_up(t, parity, f):
                no = FT * t.no + f
                if f == 0:
                    tile_there, w_there = counts(pe, CT * (t.no + 1), PARTS * (t.job + 1))
                    pe.wait_ge(tile_split, tile_there)
                    pe.wait_ge(w_split, w_there)
                pe.wait_ge(hid_done, count(pe, no - 1))
                for k, ps in ((0, gate[f % 2]), (1, up[f % 2])):
                    hi, lo = (w[t.set][k][:].rearrange("p (c n) -> p c n", c=CT) for w in (w_hi, w_lo))
                    cols = slice(P * f, P * f + P)
                    parts = [(w[:, c, cols], xp[parity][:, c, 0:t.cols]) for c in range(CT)
                             for w, xp in ((hi, t_hi), (hi, t_lo), (lo, t_hi))]
                    for m, (w, xp) in enumerate(parts):
                        ins = pe.matmul(ps[:, 0:t.cols], w, xp, start=(m == 0), stop=(m == len(parts) - 1))
                ins.then_inc(gate_up_ready, 1)

            def down(t, parity, f):
                no = FT * t.no + f
                split, left = counts(pe, no + 1, t.no - 1)
                pe.wait_ge(hid_split, split)
                if f == 0:
                    pe.wait_ge(y_done, left)
                hi, lo = (w[t.set][2][:, C * f:C * f + C] for w in (w_hi, w_lo))
                for r in range(t.rows):
                    rows = slice(P * r, P * r + P)
                    parts = ((h_hi[f % 4][:, rows], hi), (h_hi[f % 4][:, rows], lo), (h_lo[f % 4][:, rows], hi))
                    for m, (h, w) in enumerate(parts):
                        ins = pe.matmul(y_ps[parity][:, C * r:C * r + C], h, w,
                                        start=(f == 0 and m == 0 and r % 2 == 0),
                                        stop=(f == FT - 1 and m == 2), skip_group_check=True)
                ins.then_inc(hid_used, 1)

            def tile(before, t, after, parity, pieces, job):
                for f in range(FT):
                    gate_up(t, parity, f)
                    if f >= 2:
                        down(t, parity, f - 2)
                    elif before:
                        down(before, 1 - parity, FT - 2 + f)
                    if f == 4 and after and after.kind == "expert":
                        transposes(after, 1 - parity)

            all_tiles(pe, tile)
            for f in (FT - 2, FT - 1):
                down(Tile("last", NB - 1), 1, f)


def program(nc, x, w_qkv, b_qkv, w_proj, b_proj, router_w, rg, ru, rd, sg, su, sd, out):
    x1_dram = nc.dram_tensor("x1_rows", [TOKENS, C], F32, kind="Internal").ap()
    x2t_dram = nc.dram_tensor("x2_transposed", [C, TOKENS], F32, kind="Internal").ap()
    slots_dram = nc.dram_tensor("slots", [SLOTS, C], F32, kind="Internal").ap()
    rows_dram = nc.dram_tensor("expert_rows", [SLOTS + 1, C], F32, kind="Internal").ap()
    recip_dram = nc.dram_tensor("recips", [2, GRP, SEQ], F32, kind="Internal").ap()
    with ExitStack() as ctx:
        def sb(name, shape, dt=F32):
            return ctx.enter_context(nc.sbuf_tensor(name, shape, dt))

        keep = {
            "ident": sb("ident", [P, P]),
            "xn2": sb("xn2", [P, TT, C]),
            "sent_row_no": sb("sent_row_no", [P, 2, TT], U32),
            "row_no": sb("kept_row_no", [P, NB, 2, TT], U32),
            "choice_w": sb("kept_choice_w", [P, NB, 2, TT]),
            "raw": [[sb("raw0_g", [P, CT, IR]), sb("raw0_u", [P, CT, IR]), sb("raw0_d", [P, FT, C])]],
            "w_hi": [[sb(f"w_hi0_{k}", [P, CT * IR], F32R) for k in range(3)]],
            "w_lo": [[sb(f"w_lo0_{k}", [P, CT * IR], F32R) for k in range(3)]],
        }
        for name in ("raw_loaded", "w_hi_done", "w_split", "rows_sent"):
            keep[name] = ctx.enter_context(nc.semaphore(name))
        attention_block(nc, x, w_qkv, b_qkv, w_proj, b_proj, router_w, sg, su, sd,
                        x1_dram, x2t_dram, slots_dram, rows_dram, recip_dram, keep)
        ffn_block(nc, sg, su, sd, rg, ru, rd, x1_dram, x2t_dram, slots_dram, rows_dram, keep, out)


_INS = ["L0_attn_x", "L0_attn_w_qkv", "L0_attn_b_qkv", "L0_attn_w_proj", "L0_attn_b_proj", "L0_ffn_router_w",
        "L0_ffn_rg", "L0_ffn_ru", "L0_ffn_rd", "L0_ffn_sg", "L0_ffn_su", "L0_ffn_sd"]


def kernel(**inputs):
    import numpy as np
    import concourse.bacc as bacc
    from concourse.bass_utils import run_bass_kernel_spmd

    nc = bacc.Bacc("TRN2", target_bir_lowering=False, num_devices=1)
    arrays, args = {}, []
    for name in _INS:
        a = np.ascontiguousarray(inputs[name])
        arrays[f"in_{name}"] = a
        args.append(nc.dram_tensor(f"in_{name}", a.shape, mybir.dt.from_np(a.dtype), kind="ExternalInput").ap())
    args.append(nc.dram_tensor("block_out", (NB, SEQ, C), F32, kind="ExternalOutput").ap())
    program(nc, *args)
    r = run_bass_kernel_spmd(nc, [arrays], core_ids=[0])
    return r.results[0]["block_out"]
```
